# Optimizing a Trainium2 kernel written in Bass

```python
import numpy as np
import jax
import jax.numpy as jnp

def _softmax(x, axis=-1):
    return jax.nn.softmax(x, axis=axis)

def _gelu(x):
    return jax.nn.gelu(x, approximate=True)

def _silu(x):
    return jax.nn.silu(x)

def _sigmoid(x):
    return jax.nn.sigmoid(x)

def _layernorm(x, axis=-1, eps=1e-05):
    m = jnp.mean(x, axis=axis, keepdims=True)
    v = jnp.var(x, axis=axis, keepdims=True)
    return (x - m) / jnp.sqrt(v + eps)

def _scatter_add(tgt, idx, src, axis=0):
    return tgt.at[idx].add(src)

def _segment_sum(src, seg, n):
    return jax.ops.segment_sum(src, seg, n)
kernel_name = 'mk_flamingo_gated_d1_seqx_r8_543a25'

def setup_inputs(seed: int=0):
    np.random.seed(seed)
    _w = jnp.asarray

    def _rec_inputs():
        import jax
        import jax.numpy as jnp
        _rk = jax.random.key(seed)
        x = 7.22e-05 + 1 * jax.random.normal(jax.random.fold_in(_rk, 1), (128, 64, 128), jnp.float32)
        _lenS = 64 - jax.random.randint(jax.random.fold_in(_rk, 7), (128,), 0, max(1, 64 // 4) + 1, jnp.int32)
        _lenS2 = 64 - jax.random.randint(jax.random.fold_in(_rk, 8), (128,), 0, max(1, 64 // 4) + 1, jnp.int32)
        _ctx_1024P = jax.random.normal(jax.random.fold_in(_rk, 11), (128, 16, 128), jnp.float32)
        _ctx_1024c = jax.random.dirichlet(jax.random.fold_in(_rk, 511), 0.3 * jnp.ones((16,), jnp.float32), (128, 64))
        _ctx_1024t = jnp.einsum('bsk,bkd->bsd', _ctx_1024c, _ctx_1024P)
        _ctx_1024t = _ctx_1024t * jax.lax.rsqrt(jnp.mean(jnp.square(_ctx_1024t)) + 1e-12) * 0.953939
        ctx_1024 = 4.13588e-05 + 0.999923 * (_ctx_1024t + 0.3 * jax.random.normal(jax.random.fold_in(_rk, 611), (128, 64, 128), jnp.float32))
        _validS = jnp.arange(64)[None, :] < _lenS[:, None]
        _validS2 = jnp.arange(64)[None, :] < _lenS2[:, None]
        _causal = jnp.tril(jnp.ones((64, 64), dtype=bool))
        mask_BxSxS2_bk1 = jnp.broadcast_to(_validS2[:, None, :], (128, 64, 64))
        _g = jax.random.normal(jax.random.fold_in(_rk, 9001), (2, 1), jnp.float32)
        _g = jnp.sign(_g) * jnp.maximum(jnp.abs(_g), 1.0) + (_g == 0) * 1.0
        g_xattn = _g[0]
        g_ffn = _g[1]
        return (x, ctx_1024, mask_BxSxS2_bk1, g_xattn, g_ffn)
    x, ctx_1024, mask_BxSxS2_bk1, g_xattn, g_ffn = _rec_inputs()

    def _L0_xattn_setup():
        import jax, jax.numpy as jnp
        import numpy as np
        DIM_IN, DIM_Q, DIM_V = (128, 128, 128)
        B, S = (4, 256)
        NEG_INF = 1000000000.0
        key = jax.random.key(seed)
        ks = jax.random.split(key, 11)
        c_q = (6.0 / (DIM_IN + DIM_Q)) ** 0.5
        c_v = (6.0 / (DIM_IN + DIM_V)) ** 0.5
        b_bound = 1.0 / np.sqrt(DIM_IN)
        return {'query': jax.random.normal(ks[0], (B, S, DIM_IN), jnp.float32), 'key': jax.random.normal(ks[1], (B, S, DIM_IN), jnp.float32), 'value': jax.random.normal(ks[2], (B, S, DIM_IN), jnp.float32), 'mask': jax.random.randint(ks[3], (B, S, S), 0, 2).astype(bool), 'Wq': jax.random.uniform(ks[4], (DIM_Q, DIM_IN), jnp.float32, -c_q, c_q), 'bq': jax.random.uniform(ks[5], (DIM_Q,), jnp.float32, -b_bound, b_bound), 'Wk': jax.random.uniform(ks[6], (DIM_Q, DIM_IN), jnp.float32, -c_q, c_q), 'bk': jax.random.uniform(ks[7], (DIM_Q,), jnp.float32, -b_bound, b_bound), 'Wv': jax.random.uniform(ks[8], (DIM_V, DIM_IN), jnp.float32, -c_v, c_v), 'bv': jax.random.uniform(ks[9], (DIM_V,), jnp.float32, -b_bound, b_bound)}
    _L0_xattn_all = _L0_xattn_setup()
    _L0_xattn_in = {k: v for k, v in _L0_xattn_all.items() if k in ('Wq', 'bq', 'Wk', 'bk', 'Wv', 'bv')}
    del _L0_xattn_all

    def _L0_ffn_setup():
        import jax, jax.numpy as jnp
        import numpy as np
        NUM_EXPERTS = 8
        TOP_K = 2
        ROUTE_SCALE = 1.0
        DIM = 128
        HID = 128
        B, S = (2, 512)
        key = jax.random.key(seed)
        ks = jax.random.split(key, 9)
        sc = 0.05
        return {'x': jax.random.normal(ks[0], (B, S, DIM), dtype=jnp.float32), 'gate_w': jax.random.normal(ks[1], (NUM_EXPERTS, DIM), dtype=jnp.float32) * sc, 'w1': jax.random.normal(ks[2], (NUM_EXPERTS, HID, DIM), dtype=jnp.float32) * sc, 'w2': jax.random.normal(ks[3], (NUM_EXPERTS, DIM, HID), dtype=jnp.float32) * sc, 'w3': jax.random.normal(ks[4], (NUM_EXPERTS, HID, DIM), dtype=jnp.float32) * sc, 'sw1': jax.random.normal(ks[5], (HID, DIM), dtype=jnp.float32) * sc, 'sw2': jax.random.normal(ks[6], (DIM, HID), dtype=jnp.float32) * sc, 'sw3': jax.random.normal(ks[7], (HID, DIM), dtype=jnp.float32) * sc, 'expert_bias': jnp.zeros((NUM_EXPERTS,), dtype=jnp.float32)}
    _L0_ffn_all = _L0_ffn_setup()
    _L0_ffn_in = {k: v for k, v in _L0_ffn_all.items() if k in ('gate_w', 'w1', 'w2', 'w3', 'sw1', 'sw2', 'sw3', 'expert_bias')}
    del _L0_ffn_all
    return {'x': x, 'ctx_1024': ctx_1024, 'mask_BxSxS2_bk1': mask_BxSxS2_bk1, 'g_xattn': g_xattn, 'g_ffn': g_ffn, 'L0_xattn_Wq': _L0_xattn_in['Wq'], 'L0_xattn_bq': _L0_xattn_in['bq'], 'L0_xattn_Wk': _L0_xattn_in['Wk'], 'L0_xattn_bk': _L0_xattn_in['bk'], 'L0_xattn_Wv': _L0_xattn_in['Wv'], 'L0_xattn_bv': _L0_xattn_in['bv'], 'L0_ffn_gate_w': _L0_ffn_in['gate_w'], 'L0_ffn_w1': _L0_ffn_in['w1'], 'L0_ffn_w2': _L0_ffn_in['w2'], 'L0_ffn_w3': _L0_ffn_in['w3'], 'L0_ffn_sw1': _L0_ffn_in['sw1'], 'L0_ffn_sw2': _L0_ffn_in['sw2'], 'L0_ffn_sw3': _L0_ffn_in['sw3'], 'L0_ffn_expert_bias': _L0_ffn_in['expert_bias']}

def reference(x, ctx_1024, mask_BxSxS2_bk1, g_xattn, g_ffn, L0_xattn_Wq, L0_xattn_bq, L0_xattn_Wk, L0_xattn_bk, L0_xattn_Wv, L0_xattn_bv, L0_ffn_gate_w, L0_ffn_w1, L0_ffn_w2, L0_ffn_w3, L0_ffn_sw1, L0_ffn_sw2, L0_ffn_sw3, L0_ffn_expert_bias):
    import jax
    import jax.numpy as jnp

    def _L0_xattn_ref(query, key, value, mask, Wq, bq, Wk, bk, Wv, bv):
        import jax, jax.numpy as jnp
        import numpy as np
        DIM_IN, DIM_Q, DIM_V = (128, 128, 128)
        B, S = (4, 256)
        NEG_INF = 1000000000.0
        q = jnp.einsum('bsd,qd->bsq', query, Wq) + bq
        k = jnp.einsum('bsd,qd->bsq', key, Wk) + bk
        v = jnp.einsum('bsd,vd->bsv', value, Wv) + bv
        scale = 1.0 / jnp.sqrt(jnp.asarray(q.shape[-1], q.dtype))
        scores = jnp.einsum('bqd,bkd->bqk', q, k) * scale
        scores = jnp.where(mask, -NEG_INF, scores)
        affinity = jax.nn.softmax(scores, axis=-1)
        out = jnp.einsum('bqk,bkv->bqv', affinity, v)
        return out

    def _L0_ffn_ref(x, gate_w, w1, w2, w3, sw1, sw2, sw3, expert_bias):
        import jax, jax.numpy as jnp
        import numpy as np
        NUM_EXPERTS = 8
        TOP_K = 2
        ROUTE_SCALE = 1.0
        DIM = 128
        HID = 128
        B, S = (2, 512)
        bs, slen, dim = x.shape
        xf = x.reshape(-1, dim)
        scores = jax.nn.sigmoid((xf @ gate_w.T).astype(jnp.float32))
        _, sel = jax.lax.top_k(scores + expert_bias[None, :], TOP_K)
        top_scores = jnp.take_along_axis(scores, sel, axis=1) * ROUTE_SCALE
        flat_sel = sel.reshape(-1)
        order = jnp.argsort(flat_sel, stable=True)
        scores_sorted = top_scores.reshape(-1)[order]
        tok_idx = order // TOP_K
        expert_ids = flat_sel[order]
        routed = xf[tok_idx]
        routed = (routed.astype(jnp.float32) * scores_sorted[:, None]).astype(x.dtype)
        out_r = jnp.zeros_like(routed)
        for e in range(NUM_EXPERTS):
            m = (expert_ids == e)[:, None]
            h = jax.nn.silu(routed @ w1[e].T) * (routed @ w3[e].T)
            out_r = out_r + jnp.where(m, h @ w2[e].T, jnp.zeros((), routed.dtype))
        shared = jax.nn.silu(xf @ sw1.T) * (xf @ sw3.T) @ sw2.T
        out_r = (out_r.astype(jnp.float32) * scores_sorted[:, None]).astype(x.dtype)
        out = shared.at[tok_idx].add(out_r)
        return out.reshape(bs, slen, dim)
    x = x + jnp.tanh(g_xattn[0]) * _L0_xattn_ref(_layernorm(x, axis=-1), ctx_1024, ctx_1024, mask_BxSxS2_bk1, L0_xattn_Wq, L0_xattn_bq, L0_xattn_Wk, L0_xattn_bk, L0_xattn_Wv, L0_xattn_bv)
    x = x + jnp.tanh(g_ffn[0]) * _L0_ffn_ref(_layernorm(x, axis=-1), L0_ffn_gate_w, L0_ffn_w1, L0_ffn_w2, L0_ffn_w3, L0_ffn_sw1, L0_ffn_sw2, L0_ffn_sw3, L0_ffn_expert_bias)
    return x

_drawn_inputs = setup_inputs


def setup_inputs(seed=0):
    import zlib

    import numpy as np

    out = dict(_drawn_inputs(seed))
    spreads = {'L0_ffn_expert_bias': (0.0, 0.345)}
    factors = {'L0_xattn_bq': 5.395, 'L0_xattn_bk': 64.0, 'L0_ffn_gate_w': 3.495}
    for name, (base, spread) in spreads.items():
        noise = np.random.default_rng([zlib.crc32(name.encode()), seed]).standard_normal(out[name].shape)
        drawn = base * np.exp(spread * noise) if base else spread * noise
        out[name] = jnp.asarray(drawn.astype(out[name].dtype))
    for name, factor in factors.items():
        out[name] = (out[name] * factor).astype(out[name].dtype)
    return out
```

```python
from contextlib import ExitStack

import numpy as np

import concourse.bass as bass
from concourse import mybir

F32 = mybir.dt.float32
F32R = mybir.dt.float32r
U8 = mybir.dt.uint8
ALU = mybir.AluOpType
ACT = mybir.ActivationFunctionType
X = mybir.AxisListType.X

P = 128
BATCHES, SEQ, DIM = 128, 64, 128
EXPERTS, TOP_K = 8, 2
TOKENS = BATCHES * SEQ
TILE = P
TILES = 4
GROUP = TILES * TILE
GROUPS = TOKENS // GROUP
PAIR = TILE // SEQ
HALVES = 2
PER_HALF = EXPERTS // HALVES
SHARED = EXPERTS
SHARED_COLS = 2 * DIM + EXPERTS
EPS = 1e-5
SCALE = float(np.float32(1.0) / np.sqrt(np.float32(DIM)))
MASKED = -1e9 / SCALE

W13 = 0
W2 = W13 + 2 * EXPERTS * DIM
WSH = W2 + EXPERTS * DIM
WSH2 = WSH + SHARED_COLS
WCOLS = WSH2 + DIM


class Queue:

    def __init__(self):
        self.steps = []
        self.seen = {}

    def wait(self, *marks):
        for sem, value in marks:
            if self.seen.get(id(sem), 0) < value:
                self.seen[id(sem)] = value
                self.steps.append(lambda eng, s=sem, v=value: eng.wait_ge(s.handle, v))

    def do(self, instruction):
        self.steps.append(instruction)

    def make(self, sem, instruction, by=1):
        sem.value += by
        self.steps.append(lambda eng: instruction(eng).then_inc(sem.handle, by))
        return (sem, sem.value)

    def play(self, eng):
        for step in self.steps:
            step(eng)


class Counter:

    def __init__(self, handle):
        self.handle = handle
        self.value = 0


class Slot:

    def __init__(self, ap):
        self.ap = ap
        self.readers = []


def build(nc, x, ctx_t, mask, w_qkv, b_qk, bv_row, bias_row, gates, w_moe, out):
    stack = ExitStack()
    with stack:
        def sb(name, shape, dt=F32):
            return stack.enter_context(nc.sbuf_tensor(name, shape, dt))

        def sem(name):
            return Counter(stack.enter_context(nc.semaphore(name)))

        def ring(name, n, shape, dt=F32):
            whole = sb(name, [P, n] + shape, dt)
            return [Slot(whole[:, i]) for i in range(n)]

        rows = sb("rows", [P, GROUPS * TILES, DIM])
        ctx_in = ring("ctx_in", 3, [GROUP])
        ctx_hi, ctx_lo = ring("ctx_hi", 2, [GROUP], F32R), ring("ctx_lo", 2, [GROUP], F32R)
        normed = ring("normed", 2, [TILES, DIM])
        nT_hi, nT_lo = ring("nT_hi", 2, [GROUP], F32R), ring("nT_lo", 2, [GROUP], F32R)
        qT, kT = ring("qT", 2, [GROUP]), ring("kT", 2, [GROUP])
        vals = ring("vals", 3, [TILES, DIM])
        scores = ring("scores", 2, [TILES, SEQ])
        probs = ring("probs", 2, [TILES, SEQ])
        diag = ring("diag", 2, [TILES, TILE])
        diagT = ring("diagT", 2, [TILES, TILE])
        y_sb = ring("y_sb", 1, [GROUP])
        act = ring("act", 3, [PER_HALF, DIM])
        hid = ring("hid", 4, [PER_HALF, DIM])
        raw = sb("raw", [P, WCOLS])
        w_hi, w_lo = sb("w_hi", [P, WCOLS], F32R), sb("w_lo", [P, WCOLS], F32R)
        hT_hi, hT_lo = sb("hT_hi", [P, EXPERTS + 2, GROUP], F32R), sb("hT_lo", [P, EXPERTS + 2, GROUP], F32R)
        qkv_raw = sb("qkv_raw", [P, 3 * DIM])
        qkv_hi, qkv_lo = sb("qkv_hi", [P, 3 * DIM], F32R), sb("qkv_lo", [P, 3 * DIM], F32R)
        bqk = sb("bqk", [P, 2])
        bv_all = sb("bv_all", [P, DIM])
        bias_all = sb("bias_all", [P, EXPERTS])
        gate_in, gate_t = sb("gate_in", [P, 2]), sb("gate_t", [P, 2])
        mask_sb = sb("mask_sb", [P, GROUPS * TILES, SEQ], U8)
        keep = sb("keep", [P, GROUPS * TILES, SEQ], U8)
        ident = sb("ident", [P, P])
        lower, upper = sb("lower", [P, TILES, EXPERTS, EXPERTS]), sb("upper", [P, TILES, EXPERTS, EXPERTS])
        own_half, gate_own = sb("own_half", [P, PAIR]), sb("gate_own", [P, PAIR])
        neg_half = sb("neg_half", [P, TILES])
        stats = ring("stats", 2, [TILES, 6])
        moments = ring("moments", 2, [TILES, 2])
        var_eps, rstd = ring("var_eps", 2, [TILES]), ring("rstd", 2, [TILES])
        row_max, row_sum, row_inv = ring("row_max", 2, [TILES]), ring("row_sum", 2, [TILES]), ring("row_inv", 2, [TILES])
        row_scale = ring("row_scale", 2, [TILES, PAIR])
        th = ring("th", 2, [TILES, EXPERTS])
        sig = ring("sig", 2, [TILES, EXPERTS])
        ranked = ring("ranked", 2, [TILES, EXPERTS])
        over, least = ring("over", 2, [TILES, EXPERTS, EXPERTS]), ring("least", 2, [TILES, EXPERTS, EXPERTS])
        rank, chosen = ring("rank", 2, [TILES, EXPERTS]), ring("chosen", 2, [TILES, EXPERTS])
        s1, s2 = ring("s1", 2, [TILES, EXPERTS]), ring("s2", 2, [TILES, EXPERTS])
        banks = [Slot(stack.enter_context(nc.psum_tensor(f"bank{i}", [P, GROUP], F32))[:, :]) for i in range(8)]

        x_in = [sem(f"x_in{g}") for g in range(GROUPS)]
        ctx_come = [sem(f"ctx_come{i}") for i in range(3)]
        small_in, mask_in, w_in, qkv_in, gates_in = (sem(n) for n in ("small_in", "mask_in", "w_in", "qkv_in", "gates_in"))
        ident_made, tri_made, half_made, own_made, fill_made = (
            sem(n) for n in ("ident_made", "tri_made", "half_made", "own_made", "fill_made"))
        keep_made, tanh_g, gate_own_made, qkv_split_hi, qkv_split_lo, w_split_hi, w_split_lo = (
            sem(n) for n in ("keep_made", "tanh_g", "gate_own_made", "qkv_split_hi", "qkv_split_lo", "w_split_hi", "w_split_lo"))
        stats_made, moments_made, eps_added, rstd_made, normed_made = (
            sem(n) for n in ("stats_made", "moments_made", "eps_added", "rstd_made", "normed_made"))
        ctx_hi_made, ctx_lo_made = sem("ctx_hi_made"), sem("ctx_lo_made")
        nT_done, nT_hi_made, nT_lo_made = sem("nT_done"), sem("nT_hi_made"), sem("nT_lo_made")
        k_done, v_done, q_done = sem("k_done"), sem("v_done"), sem("q_done")
        k_made, v_made, q_made = sem("k_made"), sem("v_made"), sem("q_made")
        scores_done, scores_made, max_made, shifted, exp_made = (
            sem(n) for n in ("scores_done", "scores_made", "max_made", "shifted", "exp_made"))
        sum_made, inv_made, scale_made, diag_made = (sem(n) for n in ("sum_made", "inv_made", "scale_made", "diag_made"))
        diagT_done, diagT_made, attn_done, rows_made = (
            sem(n) for n in ("diagT_done", "diagT_made", "attn_done", "rows_made"))
        up_done, gate_done, act_made, prod_made, hid_made = (
            sem(n) for n in ("up_done", "gate_done", "act_made", "prod_made", "hid_made"))
        sh_done, sh_act_made, th_made, sh_hid_made = (sem(n) for n in ("sh_done", "sh_act_made", "th_made", "sh_hid_made"))
        sig_made, ranked_made, over_made, least_made, tie_made, rank_made, chosen_made, s1_made, s2_made = (
            sem(n) for n in ("sig_made", "ranked_made", "over_made", "least_made", "tie_made", "rank_made",
                             "chosen_made", "s1_made", "s2_made"))
        hT_done, hT_hi_made, hT_lo_made = sem("hT_done"), sem("hT_hi_made"), sem("hT_lo_made")
        y_done, y_made, yT_done, result_made = sem("y_done"), sem("y_made"), sem("yT_done"), sem("result_made")
        stored = sem("stored")

        sp, pe, dve, act_q, pool = Queue(), Queue(), Queue(), Queue(), Queue()

        row_of = lambda g: rows[:, TILES * g:TILES * (g + 1), :]
        x_tiles = x.rearrange("(t p) d -> p t d", p=P)
        out_tiles = out.rearrange("(t p) d -> p t d", p=P)
        x_there, ctx_there = {}, {}

        def load_x(g):
            x_there[g] = sp.make(x_in[g], lambda e: e.dma_start(row_of(g), x_tiles[:, TILES * g:TILES * (g + 1), :]), 16)

        def load_ctx(g):
            slot = ctx_in[g % 3]
            sp.wait(*slot.readers)
            ctx_there[g] = sp.make(ctx_come[g % 3], lambda e: e.dma_start(slot.ap, ctx_t[:, g * GROUP:(g + 1) * GROUP]), 16)

        load_x(0)
        load_ctx(0)
        qkv_there = sp.make(qkv_in, lambda e: e.dma_start(qkv_raw[:, :], w_qkv), 16)
        sp.make(small_in, lambda e: e.dma_start(bqk[:, :], b_qk), 16)
        sp.make(small_in, lambda e: e.dma_start(bv_all[:, :], bv_row.to_broadcast([P, DIM])), 16)
        small_there = sp.make(small_in, lambda e: e.dma_start(bias_all[:, :], bias_row.to_broadcast([P, EXPERTS])), 16)
        gates_there = sp.make(gates_in, lambda e: e.dma_start(gate_in[:, :], gates.to_broadcast([P, 2])), 16)
        load_x(1)
        load_ctx(1)
        mask_there = sp.make(mask_in, lambda e: e.dma_start(mask_sb[:, :, :], mask), 16)
        w_there = sp.make(w_in, lambda e: e.dma_start(raw[:, :], w_moe), 16)

        zeroed = pool.make(ident_made, lambda e: e.memset(ident[:, :], 0.0))
        pool.wait(zeroed)
        ident_there = pool.make(ident_made, lambda e: e.affine_select(
            out=ident[:, :], in_=ident[:, :], compare_op=ALU.not_equal, fill=1.0, base=0, pattern=[[-1, P]],
            channel_multiplier=1))
        half_there = pool.make(half_made, lambda e: e.memset(neg_half[:, :], -0.5))
        half_ones = pool.make(own_made, lambda e: e.memset(own_half[:, :], 1.0))
        pool.wait(half_ones)
        for b, (base, step) in enumerate(((SEQ - 1, -1), (-SEQ, 1))):
            own_there = pool.make(own_made, lambda e, b=b, base=base, step=step: e.affine_select(
                out=own_half[:, b:b + 1], in_=own_half[:, b:b + 1], compare_op=ALU.is_ge, fill=0.0, base=base,
                pattern=[[0, 1]], channel_multiplier=step))
        tri_made_ones = [pool.make(tri_made, lambda e, t=t: e.memset(t[:, :, :, :], 1.0)) for t in (lower, upper)]
        pool.wait(*tri_made_ones)
        for t, sign in ((lower, 1), (upper, -1)):
            tri_there = pool.make(tri_made, lambda e, t=t, sign=sign: e.affine_select(
                out=t[:, :, :, :], in_=t[:, :, :, :], compare_op=ALU.is_gt, fill=0.0, base=0,
                pattern=[[0, TILES], [sign, EXPERTS], [-sign, EXPERTS]], channel_multiplier=0))
        act_q.wait(gates_there)
        tanh_there = act_q.make(tanh_g, lambda e: e.activation(gate_t[:, :], gate_in[:, :], ACT.Tanh))
        dve.wait(tanh_there, own_there)
        gate_own_there = dve.make(gate_own_made, lambda e: e.tensor_scalar(
            gate_own[:, :], own_half[:, :], gate_t[:, 0:1], None, ALU.mult))

        def split(hi_queue, lo_queue, there, src, hi, lo, hi_sem, lo_sem):
            hi_queue.wait(*there)
            if hi_queue is act_q:
                hi_there = hi_queue.make(hi_sem, lambda e: e.activation(hi, src, ACT.Copy))
            else:
                hi_there = hi_queue.make(hi_sem, lambda e: e.tensor_copy(hi, src))
            lo_queue.wait(hi_there)
            lo_there = lo_queue.make(lo_sem, lambda e: e.tensor_tensor(lo, src, hi.bitcast(F32), ALU.subtract))
            return hi_there, lo_there

        qkv_split = split(dve, dve, [qkv_there], qkv_raw[:, :], qkv_hi[:, :], qkv_lo[:, :], qkv_split_hi, qkv_split_lo)

        def passes(w_pair, m_pair, out_ap, first=True, last=True):
            order = ((w_pair[0], m_pair[0]), (w_pair[0], m_pair[1]), (w_pair[1], m_pair[0]))
            return [lambda e, w=w, m=m, a=(first and n == 0), b=(last and n == 2): e.matmul(out_ap, w, m, start=a, stop=b)
                    for n, (w, m) in enumerate(order)]

        def run(queue, instructions, sem_=None):
            for ins in instructions[:-1]:
                queue.do(ins)
            if sem_ is None:
                queue.do(instructions[-1])
                return None
            return queue.make(sem_, instructions[-1])

        rstd_there, moments_there, normed_there = {}, {}, {}

        def norm_stats(n, g, rows_there):
            st, mo, ve, rs = (r[n % 2] for r in (stats, moments, var_eps, rstd))
            dve.wait(*rows_there)
            src = row_of(g)
            for t in range(TILES):
                made = dve.make(stats_made, lambda e, t=t: e.bn_stats(st.ap[:, t, :], src[:, t, :]))
            dve.wait(made)
            dve.wait(*mo.readers)
            for t in range(TILES):
                moments_there[n] = dve.make(moments_made, lambda e, t=t: e.bn_aggr(mo.ap[:, t, :], st.ap[:, t, :]))
            pool.wait(moments_there[n], half_there)
            pool.wait(*rs.readers)
            eps_there = pool.make(eps_added, lambda e: e.tensor_scalar(ve.ap, mo.ap[:, :, 1], EPS, None, ALU.add))
            pool.wait(eps_there)
            rstd_there[n] = pool.make(rstd_made, lambda e: e.tensor_tensor(rs.ap, ve.ap, neg_half[:, :], ALU.pow))

        def norm_apply(n, g):
            dst, mo, rs = normed[n % 2], moments[n % 2], rstd[n % 2]
            dve.wait(rstd_there[n])
            dve.wait(*dst.readers)
            src = row_of(g)
            for t in range(TILES):
                normed_there[n] = dve.make(normed_made, lambda e, t=t: e.tensor_scalar(
                    dst.ap[:, t, :], src[:, t, :], mo.ap[:, t, 0:1], rs.ap[:, t:t + 1], ALU.subtract, ALU.mult))
            mo.readers = rs.readers = [normed_there[n]]

        nT_turned = {}

        def norm_turn(n, bank):
            src = normed[n % 2]
            pe.wait(normed_there[n], ident_there)
            pe.wait(*bank.readers)
            nT_turned[n] = run(pe, [lambda e, t=t: e.transpose(bank.ap[:, t * TILE:(t + 1) * TILE], src.ap[:, t, :], ident[:, :])
                                    for t in range(TILES)], nT_done)
            src.readers = [nT_turned[n]]

        nT_there = {}

        def norm_split(n, bank):
            hi, lo = nT_hi[n % 2], nT_lo[n % 2]
            act_q.wait(*hi.readers)
            dve.wait(*lo.readers)
            nT_there[n] = split(act_q, dve, [nT_turned[n]], bank.ap, hi.ap, lo.ap, nT_hi_made, nT_lo_made)
            bank.readers = [nT_there[n][1]]

        nT_bank, q_bank, k_bank, v_bank, s_bank, dT_bank, at_bank = banks[:7]
        ctx_split, q_there, k_there, v_there, exp_there = {}, {}, {}, {}, {}
        scale_there, diag_there, diagT_there, rows_there = {}, {}, {}, {}

        def split_ctx(g):
            hi, lo, src = ctx_hi[g % 2], ctx_lo[g % 2], ctx_in[g % 3]
            act_q.wait(*hi.readers)
            pool.wait(*lo.readers)
            ctx_split[g] = split(act_q, pool, [ctx_there[g]], src.ap, hi.ap, lo.ap, ctx_hi_made, ctx_lo_made)
            src.readers = [ctx_split[g][1]]

        def project_kv(g):
            hi, lo = ctx_hi[g % 2], ctx_lo[g % 2]
            pe.wait(*qkv_split, *ctx_split[g])
            pe.wait(*k_bank.readers)
            w = (qkv_hi[:, DIM:2 * DIM], qkv_lo[:, DIM:2 * DIM])
            k_ready = run(pe, passes(w, (hi.ap, lo.ap), k_bank.ap), k_done)
            pe.wait(*v_bank.readers)
            w = (qkv_hi[:, 2 * DIM:], qkv_lo[:, 2 * DIM:])
            steps = []
            for t in range(TILES):
                at = slice(t * TILE, (t + 1) * TILE)
                steps += passes((hi.ap[:, at], lo.ap[:, at]), w, v_bank.ap[:, t * DIM:(t + 1) * DIM])
            v_ready = run(pe, steps, v_done)
            hi.readers = lo.readers = [v_ready]
            k, v = kT[g % 2], vals[g % 3]
            act_q.wait(k_ready, small_there)
            act_q.wait(*k.readers)
            k_there[g] = act_q.make(k_made, lambda e: e.activation(k.ap, k_bank.ap, ACT.Identity, bias=bqk[:, 1:2]))
            k_bank.readers = [k_there[g]]
            dve.wait(v_ready, small_there)
            dve.wait(*v.readers)
            v_there[g] = dve.make(v_made, lambda e: e.tensor_tensor(
                v.ap, v_bank.ap.rearrange("p (t d) -> p t d", t=TILES),
                bv_all[:, :].unsqueeze(1).to_broadcast([P, TILES, DIM]), ALU.add))
            v_bank.readers = [v_there[g]]

        def project_q(g):
            hi, lo, q = nT_hi[g % 2], nT_lo[g % 2], qT[g % 2]
            pe.wait(*nT_there[g])
            pe.wait(*q_bank.readers)
            q_ready = run(pe, passes((qkv_hi[:, :DIM], qkv_lo[:, :DIM]), (hi.ap, lo.ap), q_bank.ap), q_done)
            hi.readers = lo.readers = [q_ready]
            act_q.wait(q_ready)
            act_q.wait(*q.readers)
            q_there[g] = act_q.make(q_made, lambda e: e.activation(q.ap, q_bank.ap, ACT.Identity, bias=bqk[:, 0:1]))
            q_bank.readers = [q_there[g]]

        max_there, scores_ready = {}, {}

        def make_scores(g):
            q, k = qT[g % 2], kT[g % 2]
            pe.wait(q_there[g], k_there[g])
            pe.wait(*s_bank.readers)
            steps = []
            for t in range(TILES):
                for b in range(PAIR):
                    at = slice(t * TILE + b * SEQ, t * TILE + (b + 1) * SEQ)
                    steps.append(lambda e, at=at, t=t, b=b: e.matmul(
                        s_bank.ap[b * SEQ:(b + 1) * SEQ, t * SEQ:(t + 1) * SEQ], q.ap[:, at], k.ap[:, at],
                        start=True, stop=True))
            scores_ready[g] = run(pe, steps, scores_done)
            q.readers = k.readers = [scores_ready[g]]

        def mask_scores(g):
            sc, mx = scores[g % 2], row_max[g % 2]
            kept = keep[:, TILES * g:TILES * (g + 1), :]
            pool.wait(*sc.readers)
            filled = pool.make(fill_made, lambda e: e.memset(sc.ap, MASKED))
            dve.wait(mask_there)
            keep_there = dve.make(keep_made, lambda e: e.tensor_scalar(
                kept, mask_sb[:, TILES * g:TILES * (g + 1), :], 0.0, None, ALU.is_equal))
            dve.wait(scores_ready[g], filled, keep_there)
            made = dve.make(scores_made, lambda e: e.copy_predicated(
                sc.ap, kept, s_bank.ap[:, :TILES * SEQ].rearrange("p (t k) -> p t k", t=TILES)))
            s_bank.readers = [made]
            dve.wait(made)
            dve.wait(*mx.readers)
            max_there[g] = dve.make(max_made, lambda e: e.reduce_max(mx.ap, sc.ap, X))
            pool.wait(max_there[g])
            off = pool.make(shifted, lambda e: e.tensor_tensor(
                sc.ap, sc.ap, mx.ap.unsqueeze(2).to_broadcast([P, TILES, SEQ]), ALU.subtract))
            mx.readers = [off]
            pr = probs[g % 2]
            act_q.wait(off)
            act_q.wait(*pr.readers)
            exp_there[g] = act_q.make(exp_made, lambda e: e.activation(pr.ap, sc.ap, ACT.Exp, scale=SCALE))
            sc.readers = [exp_there[g]]

        def normalise(g):
            pr, sm, iv, rs, dg = probs[g % 2], row_sum[g % 2], row_inv[g % 2], row_scale[g % 2], diag[g % 2]
            dve.wait(exp_there[g])
            dve.wait(*iv.readers)
            summed = dve.make(sum_made, lambda e: e.reduce_sum(sm.ap, pr.ap, X))
            dve.wait(summed)
            inverted = dve.make(inv_made, lambda e: e.reciprocal(iv.ap, sm.ap))
            dve.wait(inverted, gate_own_there)
            dve.wait(*rs.readers)
            full = [P, TILES, PAIR]
            scale_there[g] = dve.make(scale_made, lambda e: e.tensor_tensor(
                rs.ap, iv.ap.unsqueeze(2).to_broadcast(full), gate_own[:, :].unsqueeze(1).to_broadcast(full), ALU.mult))
            iv.readers = [scale_there[g]]
            pool.wait(scale_there[g])
            pool.wait(*dg.readers)
            full4 = [P, TILES, PAIR, SEQ]
            diag_there[g] = pool.make(diag_made, lambda e: e.tensor_tensor(
                dg.ap.rearrange("p t (b k) -> p t b k", b=PAIR), pr.ap.unsqueeze(2).to_broadcast(full4),
                rs.ap.unsqueeze(3).to_broadcast(full4), ALU.mult))
            pr.readers = rs.readers = [diag_there[g]]

        def turn_probs(g):
            dg, dt = diag[g % 2], diagT[g % 2]
            pe.wait(diag_there[g])
            pe.wait(*dT_bank.readers)
            turned = run(pe, [lambda e, t=t: e.transpose(dT_bank.ap[:, t * TILE:(t + 1) * TILE], dg.ap[:, t, :], ident[:, :])
                              for t in range(TILES)], diagT_done)
            dg.readers = [turned]
            act_q.wait(turned)
            act_q.wait(*dt.readers)
            diagT_there[g] = act_q.make(diagT_made, lambda e: e.activation(
                dt.ap, dT_bank.ap.rearrange("p (t c) -> p t c", t=TILES), ACT.Copy))
            dT_bank.readers = [diagT_there[g]]

        def attend(g):
            dt, v = diagT[g % 2], vals[g % 3]
            pe.wait(diagT_there[g], v_there[g])
            pe.wait(*at_bank.readers)
            attended = run(pe, [lambda e, t=t: e.matmul(at_bank.ap[:, t * DIM:(t + 1) * DIM], dt.ap[:, t, :], v.ap[:, t, :],
                                                        start=True, stop=True) for t in range(TILES)], attn_done)
            dt.readers = v.readers = [attended]
            dve.wait(attended, normed_there[g])
            rows_there[g] = dve.make(rows_made, lambda e: e.tensor_tensor(
                row_of(g), row_of(g), at_bank.ap.rearrange("p (t d) -> p t d", t=TILES), ALU.add))
            at_bank.readers = [rows_there[g]]

        w_split = {}

        def split_weights(c):
            at = slice(c * GROUP, min((c + 1) * GROUP, WCOLS))
            w_split[c] = split(act_q, pool, [w_there], raw[:, at], w_hi[:, at], w_lo[:, at], w_split_hi, w_split_lo)

        for s in range(GROUPS + 3):
            now, last, before, oldest = s, s - 1, s - 2, s - 3
            has = lambda g: 0 <= g < GROUPS
            if s + 2 < GROUPS:
                load_x(s + 2)
                load_ctx(s + 2)
            if has(now):
                norm_stats(now, now, [x_there[now]])
            if has(last):
                norm_turn(last, nT_bank)
                norm_split(last, nT_bank)
            if has(oldest):
                turn_probs(oldest)
            if has(before):
                make_scores(before)
                mask_scores(before)
            if has(now):
                norm_apply(now, now)
                split_ctx(now)
            if has(last):
                project_kv(last)
            if has(before):
                normalise(before)
            if has(last):
                project_q(last)
            if has(oldest):
                attend(oldest)
            if 1 <= s and (s - 1) * GROUP < WCOLS:
                split_weights(s - 1)

        up_banks, gate_banks, hT_banks, y_bank, side_bank = banks[0:2], banks[2:4], banks[4:6], banks[6], banks[7]
        all_weights = [m for pair in w_split.values() for m in pair]
        units = 0
        th_there, sh_act_there, s1_there, s2_there, sh_hid_there = {}, {}, {}, {}, {}
        hid_count = 0

        def shared_layer1(g, pair):
            nonlocal units
            n = GROUPS + g
            hi, lo = nT_hi[n % 2], nT_lo[n % 2]
            u = units
            units += 1
            pe.wait(*nT_there[n], *all_weights)
            ac, hd = act[act_turn(g, pair)], sh_hid[g % 2]
            for i in range(2):
                t = 2 * pair + i
                bank = (up_banks, gate_banks)[i][u % 2]
                at = slice(t * TILE, (t + 1) * TILE)
                out_ap = bank.ap[:, :SHARED_COLS]
                pe.wait(*bank.readers)
                w = slice(WSH, WSH + SHARED_COLS)
                ready = run(pe, passes((hi.ap[:, at], lo.ap[:, at]), (w_hi[:, w], w_lo[:, w]), out_ap), sh_done)
                act_q.wait(ready)
                act_q.wait(*ac.readers)
                if t == 0:
                    act_q.wait(*th[g % 2].readers)
                th_there[g] = act_q.make(th_made, lambda e, bank=bank, t=t: e.activation(
                    th[g % 2].ap[:, t, :], bank.ap[:, 2 * DIM:SHARED_COLS], ACT.Tanh, scale=0.5))
                silu = act_q.make(sh_act_made, lambda e, bank=bank, i=i: e.activation(
                    ac.ap[:, i, :], bank.ap[:, :DIM], ACT.Silu))
                dve.wait(silu)
                if t == 0:
                    dve.wait(*hd.readers)
                sh_hid_there[g] = dve.make(sh_hid_made, lambda e, bank=bank, i=i, t=t: e.tensor_tensor(
                    hd.ap[:, t, :], ac.ap[:, i, :], bank.ap[:, DIM:2 * DIM], ALU.mult))
                bank.readers = [sh_hid_there[g]]
            ac.readers = [sh_hid_there[g]]

        turns = 0

        def act_turn(*_):
            nonlocal turns
            turns += 1
            return (turns - 1) % 3

        sh_hid = ring("sh_hid", 2, [TILES, DIM])

        def route(g):
            i = g % 2
            dve.wait(th_there[g])
            dve.wait(*sig[i].readers)
            a = dve.make(sig_made, lambda e: e.tensor_scalar(sig[i].ap, th[i].ap, 0.5, 0.5, ALU.mult, ALU.add))
            th[i].readers = [a]
            dve.wait(a, small_there)
            b = dve.make(ranked_made, lambda e: e.tensor_tensor(
                ranked[i].ap, sig[i].ap, bias_all[:, :].unsqueeze(1).to_broadcast([P, TILES, EXPERTS]), ALU.add))
            dve.wait(b)
            full = [P, TILES, EXPERTS, EXPERTS]
            other, own = ranked[i].ap.unsqueeze(2).to_broadcast(full), ranked[i].ap.unsqueeze(3).to_broadcast(full)
            dve.wait(*over[i].readers)
            c = dve.make(over_made, lambda e: e.tensor_tensor(over[i].ap, other, own, ALU.is_gt))
            d = dve.make(least_made, lambda e: e.tensor_tensor(least[i].ap, other, own, ALU.is_ge))
            pool.wait(c, d, tri_there)
            f = pool.make(tie_made, lambda e: e.tensor_tensor(over[i].ap, over[i].ap, upper[:, :, :, :], ALU.mult))
            h = pool.make(tie_made, lambda e: e.tensor_tensor(least[i].ap, least[i].ap, lower[:, :, :, :], ALU.mult))
            pool.wait(f, h)
            k = pool.make(tie_made, lambda e: e.tensor_tensor(over[i].ap, over[i].ap, least[i].ap, ALU.add))
            dve.wait(k)
            r = dve.make(rank_made, lambda e: e.reduce_sum(rank[i].ap, over[i].ap, X))
            over[i].readers = [r]
            dve.wait(r)
            ch = dve.make(chosen_made, lambda e: e.tensor_scalar(chosen[i].ap, rank[i].ap, float(TOP_K), None, ALU.is_lt))
            dve.wait(ch)
            dve.wait(*s1[i].readers)
            s1_there[g] = dve.make(s1_made, lambda e: e.tensor_tensor(s1[i].ap, chosen[i].ap, sig[i].ap, ALU.mult))
            sig[i].readers = [s1_there[g]]
            dve.wait(s1_there[g])
            dve.wait(*s2[i].readers)
            s2_there[g] = dve.make(s2_made, lambda e: e.tensor_tensor(s2[i].ap, s1[i].ap, s1[i].ap, ALU.mult))

        hid_there = {}

        def layer1(g, u):
            nonlocal units, hid_count
            t, half = u // HALVES, u % HALVES
            n = GROUPS + g
            hi, lo = nT_hi[n % 2], nT_lo[n % 2]
            at = slice(t * TILE, (t + 1) * TILE)
            up, gt = up_banks[units % 2], gate_banks[units % 2]
            units += 1
            pe.wait(*nT_there[n], *all_weights)
            ready = []
            for m, (bank, made) in enumerate(((up, up_done), (gt, gate_done))):
                c = W13 + (half * 2 + m) * PER_HALF * DIM
                w = slice(c, c + PER_HALF * DIM)
                pe.wait(*bank.readers)
                ready.append(run(pe, passes((hi.ap[:, at], lo.ap[:, at]), (w_hi[:, w], w_lo[:, w]), bank.ap), made))
            if u == TILES * HALVES - 1:
                hi.readers = lo.readers = [ready[1]]
            ac, hd = act[act_turn()], hid[hid_count % 4]
            hid_count += 1
            act_q.wait(ready[0], s1_there[g])
            act_q.wait(*ac.readers)
            for j in range(PER_HALF):
                e_ = half * PER_HALF + j
                silu = act_q.make(act_made, lambda e, j=j, e_=e_: e.activation(
                    ac.ap[:, j, :], up.ap[:, j * DIM:(j + 1) * DIM], ACT.Silu, scale=s1[g % 2].ap[:, t, e_:e_ + 1]))
            up.readers = [silu]
            s1[g % 2].readers = [silu]
            dve.wait(silu, ready[1])
            dve.wait(*hd.readers)
            prod = dve.make(prod_made, lambda e: e.tensor_tensor(
                hd.ap, ac.ap, gt.ap.rearrange("p (j d) -> p j d", j=PER_HALF), ALU.mult))
            ac.readers = gt.readers = [prod]
            pool.wait(prod, s2_there[g])
            es = slice(half * PER_HALF, (half + 1) * PER_HALF)
            hid_there[g, u] = pool.make(hid_made, lambda e: e.tensor_tensor(
                hd.ap, hd.ap, s2[g % 2].ap[:, t, es].unsqueeze(2).to_broadcast([P, PER_HALF, DIM]), ALU.mult))
            s2[g % 2].readers = [hid_there[g, u]]
            waiting.append((hd, hid_there[g, u], slice(half * PER_HALF, (half + 1) * PER_HALF), at, g))

        waiting, turned_count = [], 0
        hT_there = {}
        y_ready = {}

        def turn_hidden():
            nonlocal turned_count
            hd, there, slots, at, g = waiting.pop(0)
            bank = hT_banks[turned_count % 2]
            turned_count += 1
            pe.wait(there)
            pe.wait(*bank.readers)
            turned = run(pe, [lambda e, j=j: e.transpose(bank.ap[:, j * TILE:(j + 1) * TILE], hd.ap[:, j, :], ident[:, :])
                              for j in range(4)], hT_done)
            hd.readers = [turned]
            if at is None:
                hi, lo, src = hT_hi[:, slots, :], hT_lo[:, slots, :], bank.ap
                free = y_ready.get(g - 2)
            else:
                hi, lo, src = hT_hi[:, slots, at], hT_lo[:, slots, at], bank.ap.rearrange("p (j c) -> p j c", j=PER_HALF)
                free = y_ready.get(g - 1)
            if free:
                act_q.wait(free)
                dve.wait(free)
            pair = split(act_q, dve, [turned], src, hi, lo, hT_hi_made, hT_lo_made)
            bank.readers = [pair[1]]
            hT_there[g] = pair

        yT_there = {}

        def layer2(g):
            pe.wait(*hT_there[g])
            pe.wait(*y_bank.readers)
            steps = []
            order = [SHARED] + list(range(EXPERTS))
            for k, e_ in enumerate(order):
                c = WSH2 if e_ == SHARED else W2 + e_ * DIM
                slot = SHARED + g % 2 if e_ == SHARED else e_
                w = slice(c, c + DIM)
                steps += passes((w_hi[:, w], w_lo[:, w]), (hT_hi[:, slot, :], hT_lo[:, slot, :]), y_bank.ap,
                                first=(k == 0), last=(k == len(order) - 1))
            y_ready[g] = run(pe, steps, y_done)
            act_q.wait(y_ready[g], tanh_there)
            act_q.wait(*y_sb[0].readers)
            yT_there[g] = act_q.make(y_made, lambda e: e.activation(y_sb[0].ap, y_bank.ap, ACT.Copy, scale=gate_t[:, 1:2]))
            y_bank.readers = [yT_there[g]]

        def finish(g):
            pe.wait(yT_there[g])
            pe.wait(*side_bank.readers)
            turned = run(pe, [lambda e, t=t: e.transpose(side_bank.ap[:, t * DIM:(t + 1) * DIM],
                                                         y_sb[0].ap[:, t * TILE:(t + 1) * TILE], ident[:, :])
                              for t in range(TILES)], yT_done)
            y_sb[0].readers = [turned]
            dve.wait(turned, normed_there[GROUPS + g])
            made = dve.make(result_made, lambda e: e.tensor_tensor(
                row_of(g), row_of(g), side_bank.ap.rearrange("p (t d) -> p t d", t=TILES), ALU.add))
            side_bank.readers = [made]
            sp.wait(made)
            return sp.make(stored, lambda e: e.dma_start(out_tiles[:, TILES * g:TILES * (g + 1), :], row_of(g)), 16)

        def prepare(g, part):
            if g >= GROUPS:
                return
            n = GROUPS + g
            if part == 0:
                norm_stats(n, g, [rows_there[g]])
            elif part == 1:
                norm_apply(n, g)
            elif part == 2:
                norm_turn(n, side_bank)
                norm_split(n, side_bank)
            elif part == 3:
                shared_layer1(g, 0)
            elif part == 4:
                shared_layer1(g, 1)
                route(g)
                waiting.append((sh_hid[g % 2], sh_hid_there[g], SHARED + g % 2, None, g))

        for part in range(5):
            prepare(0, part)
        for g in range(GROUPS):
            for u in range(TILES * HALVES):
                layer1(g, u)
                if u == 2 and g:
                    layer2(g - 1)
                if u == 3 and g:
                    finish(g - 1)
                if u >= 1:
                    prepare(g + 1, u - 1)
                while len(waiting) > 2:
                    turn_hidden()
        while waiting:
            turn_hidden()
        layer2(GROUPS - 1)
        all_stored = finish(GROUPS - 1)
        sp.wait(all_stored)

        block = stack.enter_context(nc.Block())
        block.sync(sp.play)
        block.tensor(pe.play)
        block.vector(dve.play)
        block.scalar(act_q.play)
        block.gpsimd(pool.play)


def kernel(**inputs):
    import concourse.bacc as bacc
    from concourse.bass_utils import run_bass_kernel_spmd

    a = {k: np.asarray(v) for k, v in inputs.items()}
    down = lambda w: w.transpose(2, 0, 1)
    w1, w3 = (down(a[f"L0_ffn_w{i}"]).reshape(DIM, HALVES, PER_HALF * DIM) for i in (1, 3))
    w13 = np.stack([w1, w3], axis=2).reshape(DIM, -1)
    w_moe = np.concatenate([w13, down(a["L0_ffn_w2"]).reshape(DIM, -1), a["L0_ffn_sw1"].T, a["L0_ffn_sw3"].T,
                            a["L0_ffn_gate_w"].T, a["L0_ffn_sw2"].T], axis=1)
    arrays = {
        "x": a["x"].reshape(TOKENS, DIM),
        "ctx_t": a["ctx_1024"].reshape(TOKENS, DIM).T,
        "mask": a["mask_BxSxS2_bk1"].reshape(TOKENS // TILE, TILE, SEQ).transpose(1, 0, 2),
        "w_qkv": np.concatenate([a[f"L0_xattn_W{n}"].T for n in "qkv"], axis=1),
        "b_qk": np.stack([a["L0_xattn_bq"], a["L0_xattn_bk"]], axis=1),
        "bv_row": a["L0_xattn_bv"].reshape(1, DIM),
        "bias_row": a["L0_ffn_expert_bias"].reshape(1, EXPERTS),
        "gates": np.stack([a["g_xattn"], a["g_ffn"]], axis=1),
        "w_moe": w_moe,
    }
    arrays = {k: np.ascontiguousarray(v) for k, v in arrays.items()}
    nc = bacc.Bacc("TRN2", target_bir_lowering=False, num_devices=1)
    aps = [nc.dram_tensor(k, v.shape, mybir.dt.from_np(v.dtype), kind="ExternalInput").ap() for k, v in arrays.items()]
    out = nc.dram_tensor("out", (TOKENS, DIM), F32, kind="ExternalOutput").ap()
    build(nc, *aps, out)
    r = run_bass_kernel_spmd(nc, [arrays], core_ids=[0])
    return r.results[0]["out"].reshape(BATCHES, SEQ, DIM)
```

```python
from contextlib import ExitStack

import numpy as np

import concourse.bass as bass
from concourse import mybir

F32 = mybir.dt.float32
F32R = mybir.dt.float32r
U8 = mybir.dt.uint8
ALU = mybir.AluOpType
ACT = mybir.ActivationFunctionType
X = mybir.AxisListType.X

P = 128
BATCHES, SEQ, DIM = 128, 64, 128
EXPERTS, TOP_K = 8, 2
TOKENS = BATCHES * SEQ
TILE = P
TILES = 4
GROUP = TILES * TILE
GROUPS = TOKENS // GROUP
PAIR = TILE // SEQ
HALVES = 2
PER_HALF = EXPERTS // HALVES
SHARED = EXPERTS
SHARED_COLS = 2 * DIM + EXPERTS
EPS = 1e-5
SCALE = float(np.float32(1.0) / np.sqrt(np.float32(DIM)))
MASKED = -1e9 / SCALE

W13 = 0
W2 = W13 + 2 * EXPERTS * DIM
WSH = W2 + EXPERTS * DIM
WSH2 = WSH + SHARED_COLS
WCOLS = WSH2 + DIM


class Queue:

    def __init__(self):
        self.steps = []
        self.seen = {}

    def wait(self, *marks):
        for sem, value in marks:
            if self.seen.get(id(sem), 0) < value:
                self.seen[id(sem)] = value
                self.steps.append(lambda eng, s=sem, v=value: eng.wait_ge(s.handle, v))

    def do(self, instruction):
        self.steps.append(instruction)

    def make(self, sem, instruction, by=1):
        sem.value += by
        self.steps.append(lambda eng: instruction(eng).then_inc(sem.handle, by))
        return (sem, sem.value)

    def play(self, eng):
        for step in self.steps:
            step(eng)


class Counter:

    def __init__(self, handle):
        self.handle = handle
        self.value = 0


class Slot:

    def __init__(self, ap):
        self.ap = ap
        self.readers = []


def build(nc, x, ctx_t, mask, w_qkv, b_qk, bv_row, bias_row, gates, w_moe, out):
    stack = ExitStack()
    with stack:
        def sb(name, shape, dt=F32, scope=stack):
            return scope.enter_context(nc.sbuf_tensor(name, shape, dt))

        def sem(name):
            return Counter(stack.enter_context(nc.semaphore(name)))

        def ring(name, n, shape, dt=F32, scope=stack):
            whole = sb(name, [P, n] + shape, dt, scope)
            return [Slot(whole[:, i]) for i in range(n)]

        rows = sb("rows", [P, GROUPS * TILES, DIM])
        normed = ring("normed", 2, [TILES, DIM])
        nT_hi, nT_lo = ring("nT_hi", 2, [GROUP], F32R), ring("nT_lo", 2, [GROUP], F32R)
        y_sb = ring("y_sb", 1, [GROUP])
        act = ring("act", 3, [PER_HALF, DIM])
        hid = ring("hid", 4, [PER_HALF, DIM])
        w_hi, w_lo = sb("w_hi", [P, WCOLS], F32R), sb("w_lo", [P, WCOLS], F32R)
        bqk = sb("bqk", [P, 2])
        bv_all = sb("bv_all", [P, DIM])
        bias_all = sb("bias_all", [P, EXPERTS])
        gate_in, gate_t = sb("gate_in", [P, 2]), sb("gate_t", [P, 2])
        ident = sb("ident", [P, P])
        lower, upper = sb("lower", [P, TILES, EXPERTS, EXPERTS]), sb("upper", [P, TILES, EXPERTS, EXPERTS])
        own_half, gate_own = sb("own_half", [P, PAIR]), sb("gate_own", [P, PAIR])
        neg_half = sb("neg_half", [P, TILES])
        stats = ring("stats", 2, [TILES, 6])
        moments = ring("moments", 2, [TILES, 2])
        var_eps, rstd = ring("var_eps", 2, [TILES]), ring("rstd", 2, [TILES])
        row_max, row_sum, row_inv = ring("row_max", 2, [TILES]), ring("row_sum", 2, [TILES]), ring("row_inv", 2, [TILES])
        row_scale = ring("row_scale", 2, [TILES, PAIR])
        th = ring("th", 2, [TILES, EXPERTS])
        sig = ring("sig", 2, [TILES, EXPERTS])
        ranked = ring("ranked", 2, [TILES, EXPERTS])
        over, least = ring("over", 2, [TILES, EXPERTS, EXPERTS]), ring("least", 2, [TILES, EXPERTS, EXPERTS])
        rank, chosen = ring("rank", 2, [TILES, EXPERTS]), ring("chosen", 2, [TILES, EXPERTS])
        s1, s2 = ring("s1", 2, [TILES, EXPERTS]), ring("s2", 2, [TILES, EXPERTS])
        sh_hid = ring("sh_hid", 2, [TILES, DIM])
        attention = stack.enter_context(ExitStack())
        ctx_in = ring("ctx_in", 3, [GROUP], scope=attention)
        ctx_hi, ctx_lo = ring("ctx_hi", 2, [GROUP], F32R, scope=attention), ring("ctx_lo", 2, [GROUP], F32R, scope=attention)
        qT, kT = ring("qT", 2, [GROUP], scope=attention), ring("kT", 2, [GROUP], scope=attention)
        vals = ring("vals", 3, [TILES, DIM], scope=attention)
        scores = ring("scores", 2, [TILES, SEQ], scope=attention)
        probs = ring("probs", 2, [TILES, SEQ], scope=attention)
        diag = ring("diag", 2, [TILES, TILE], scope=attention)
        diagT = ring("diagT", 2, [TILES, TILE], scope=attention)
        raw = sb("raw", [P, WCOLS], scope=attention)
        qkv_raw = sb("qkv_raw", [P, 3 * DIM], scope=attention)
        qkv_hi, qkv_lo = sb("qkv_hi", [P, 3 * DIM], F32R, scope=attention), sb("qkv_lo", [P, 3 * DIM], F32R, scope=attention)
        mask_sb = sb("mask_sb", [P, GROUPS * TILES, SEQ], U8, scope=attention)
        keep = sb("keep", [P, GROUPS * TILES, SEQ], U8, scope=attention)
        attention.close()
        hT_hi, hT_lo = ring("hT_hi", 2, [EXPERTS + 1, GROUP], F32R), ring("hT_lo", 2, [EXPERTS + 1, GROUP], F32R)
        banks = [Slot(stack.enter_context(nc.psum_tensor(f"bank{i}", [P, GROUP], F32))[:, :]) for i in range(8)]

        x_in = [sem(f"x_in{g}") for g in range(GROUPS)]
        ctx_come = [sem(f"ctx_come{i}") for i in range(3)]
        small_in, mask_in, w_in, qkv_in, gates_in = (sem(n) for n in ("small_in", "mask_in", "w_in", "qkv_in", "gates_in"))
        ident_made, tri_made, half_made, own_made, fill_made = (
            sem(n) for n in ("ident_made", "tri_made", "half_made", "own_made", "fill_made"))
        keep_made, tanh_g, gate_own_made, qkv_split_hi, qkv_split_lo, w_split_hi, w_split_lo = (
            sem(n) for n in ("keep_made", "tanh_g", "gate_own_made", "qkv_split_hi", "qkv_split_lo", "w_split_hi", "w_split_lo"))
        stats_made, moments_made, eps_added, rstd_made, normed_made = (
            sem(n) for n in ("stats_made", "moments_made", "eps_added", "rstd_made", "normed_made"))
        ctx_hi_made, ctx_lo_made = sem("ctx_hi_made"), sem("ctx_lo_made")
        nT_done, nT_hi_made, nT_lo_made = sem("nT_done"), sem("nT_hi_made"), sem("nT_lo_made")
        k_done, v_done, q_done = sem("k_done"), sem("v_done"), sem("q_done")
        k_made, v_made, q_made = sem("k_made"), sem("v_made"), sem("q_made")
        scores_done, scores_made, max_made, shifted, exp_made = (
            sem(n) for n in ("scores_done", "scores_made", "max_made", "shifted", "exp_made"))
        sum_made, inv_made, scale_made, diag_made = (sem(n) for n in ("sum_made", "inv_made", "scale_made", "diag_made"))
        diagT_done, diagT_made, attn_done, rows_made = (
            sem(n) for n in ("diagT_done", "diagT_made", "attn_done", "rows_made"))
        up_done, gate_done, act_made, prod_made, hid_made = (
            sem(n) for n in ("up_done", "gate_done", "act_made", "prod_made", "hid_made"))
        sh_done, sh_act_made, th_made, sh_hid_made = (sem(n) for n in ("sh_done", "sh_act_made", "th_made", "sh_hid_made"))
        sig_made, ranked_made, over_made, least_made, tie_made, rank_made, chosen_made, s1_made, s2_made = (
            sem(n) for n in ("sig_made", "ranked_made", "over_made", "least_made", "tie_made", "rank_made",
                             "chosen_made", "s1_made", "s2_made"))
        hT_done, hT_hi_made, hT_lo_made = sem("hT_done"), sem("hT_hi_made"), sem("hT_lo_made")
        y_done, y_made, yT_done, result_made = sem("y_done"), sem("y_made"), sem("yT_done"), sem("result_made")
        stored = sem("stored")

        sp, pe, dve, act_q, pool = Queue(), Queue(), Queue(), Queue(), Queue()

        row_of = lambda g: rows[:, TILES * g:TILES * (g + 1), :]
        x_tiles = x.rearrange("(t p) d -> p t d", p=P)
        out_tiles = out.rearrange("(t p) d -> p t d", p=P)
        x_there, ctx_there = {}, {}

        def load_x(g):
            x_there[g] = sp.make(x_in[g], lambda e: e.dma_start(row_of(g), x_tiles[:, TILES * g:TILES * (g + 1), :]), 16)

        def load_ctx(g):
            slot = ctx_in[g % 3]
            sp.wait(*slot.readers)
            ctx_there[g] = sp.make(ctx_come[g % 3], lambda e: e.dma_start(slot.ap, ctx_t[:, g * GROUP:(g + 1) * GROUP]), 16)

        load_x(0)
        load_ctx(0)
        qkv_there = sp.make(qkv_in, lambda e: e.dma_start(qkv_raw[:, :], w_qkv), 16)
        sp.make(small_in, lambda e: e.dma_start(bqk[:, :], b_qk), 16)
        sp.make(small_in, lambda e: e.dma_start(bv_all[:, :], bv_row.to_broadcast([P, DIM])), 16)
        small_there = sp.make(small_in, lambda e: e.dma_start(bias_all[:, :], bias_row.to_broadcast([P, EXPERTS])), 16)
        gates_there = sp.make(gates_in, lambda e: e.dma_start(gate_in[:, :], gates.to_broadcast([P, 2])), 16)
        load_x(1)
        load_ctx(1)
        mask_there = sp.make(mask_in, lambda e: e.dma_start(mask_sb[:, :, :], mask), 16)
        w_there = sp.make(w_in, lambda e: e.dma_start(raw[:, :], w_moe), 16)

        zeroed = pool.make(ident_made, lambda e: e.memset(ident[:, :], 0.0))
        pool.wait(zeroed)
        ident_there = pool.make(ident_made, lambda e: e.affine_select(
            out=ident[:, :], in_=ident[:, :], compare_op=ALU.not_equal, fill=1.0, base=0, pattern=[[-1, P]],
            channel_multiplier=1))
        half_there = pool.make(half_made, lambda e: e.memset(neg_half[:, :], -0.5))
        half_ones = pool.make(own_made, lambda e: e.memset(own_half[:, :], 1.0))
        pool.wait(half_ones)
        for b, (base, step) in enumerate(((SEQ - 1, -1), (-SEQ, 1))):
            own_there = pool.make(own_made, lambda e, b=b, base=base, step=step: e.affine_select(
                out=own_half[:, b:b + 1], in_=own_half[:, b:b + 1], compare_op=ALU.is_ge, fill=0.0, base=base,
                pattern=[[0, 1]], channel_multiplier=step))
        tri_made_ones = [pool.make(tri_made, lambda e, t=t: e.memset(t[:, :, :, :], 1.0)) for t in (lower, upper)]
        pool.wait(*tri_made_ones)
        for t, sign in ((lower, 1), (upper, -1)):
            tri_there = pool.make(tri_made, lambda e, t=t, sign=sign: e.affine_select(
                out=t[:, :, :, :], in_=t[:, :, :, :], compare_op=ALU.is_gt, fill=0.0, base=0,
                pattern=[[0, TILES], [sign, EXPERTS], [-sign, EXPERTS]], channel_multiplier=0))
        act_q.wait(gates_there)
        tanh_there = act_q.make(tanh_g, lambda e: e.activation(gate_t[:, :], gate_in[:, :], ACT.Tanh))
        dve.wait(tanh_there, own_there)
        gate_own_there = dve.make(gate_own_made, lambda e: e.tensor_scalar(
            gate_own[:, :], own_half[:, :], gate_t[:, 0:1], None, ALU.mult))

        def split(hi_queue, lo_queue, there, src, hi, lo, hi_sem, lo_sem):
            hi_queue.wait(*there)
            if hi_queue is act_q:
                hi_there = hi_queue.make(hi_sem, lambda e: e.activation(hi, src, ACT.Copy))
            else:
                hi_there = hi_queue.make(hi_sem, lambda e: e.tensor_copy(hi, src))
            lo_queue.wait(hi_there)
            lo_there = lo_queue.make(lo_sem, lambda e: e.tensor_tensor(lo, src, hi.bitcast(F32), ALU.subtract))
            return hi_there, lo_there

        qkv_split = split(dve, dve, [qkv_there], qkv_raw[:, :], qkv_hi[:, :], qkv_lo[:, :], qkv_split_hi, qkv_split_lo)

        def passes(w_pair, m_pair, out_ap, first=True, last=True):
            order = ((w_pair[0], m_pair[0]), (w_pair[0], m_pair[1]), (w_pair[1], m_pair[0]))
            return [lambda e, w=w, m=m, a=(first and n == 0), b=(last and n == 2): e.matmul(out_ap, w, m, start=a, stop=b)
                    for n, (w, m) in enumerate(order)]

        def run(queue, instructions, sem_=None):
            for ins in instructions[:-1]:
                queue.do(ins)
            if sem_ is None:
                queue.do(instructions[-1])
                return None
            return queue.make(sem_, instructions[-1])

        chores = []

        def finish_chore(chore):
            for _ in chore:
                pass

        def drip():
            if chores:
                try:
                    next(chores[0])
                except StopIteration:
                    chores.pop(0)
                    drip()

        rstd_there, moments_there, normed_there = {}, {}, {}

        def norm_stats(n, g, rows_there):
            st, mo, ve, rs = (r[n % 2] for r in (stats, moments, var_eps, rstd))
            dve.wait(*rows_there)
            src = row_of(g)
            for t in range(TILES):
                if t == 2:
                    yield
                made = dve.make(stats_made, lambda e, t=t: e.bn_stats(st.ap[:, t, :], src[:, t, :]))
            yield
            dve.wait(made)
            dve.wait(*mo.readers)
            for t in range(TILES):
                moments_there[n] = dve.make(moments_made, lambda e, t=t: e.bn_aggr(mo.ap[:, t, :], st.ap[:, t, :]))
            pool.wait(moments_there[n], half_there)
            pool.wait(*rs.readers)
            eps_there = pool.make(eps_added, lambda e: e.tensor_scalar(ve.ap, mo.ap[:, :, 1], EPS, None, ALU.add))
            pool.wait(eps_there)
            rstd_there[n] = pool.make(rstd_made, lambda e: e.tensor_tensor(rs.ap, ve.ap, neg_half[:, :], ALU.pow))
            yield

        def norm_apply(n, g):
            dst, mo, rs = normed[n % 2], moments[n % 2], rstd[n % 2]
            dve.wait(rstd_there[n])
            dve.wait(*dst.readers)
            src = row_of(g)
            for t in range(TILES):
                if t == 2:
                    yield
                normed_there[n] = dve.make(normed_made, lambda e, t=t: e.tensor_scalar(
                    dst.ap[:, t, :], src[:, t, :], mo.ap[:, t, 0:1], rs.ap[:, t:t + 1], ALU.subtract, ALU.mult))
            mo.readers = rs.readers = [normed_there[n]]
            yield

        nT_turned = {}

        def norm_turn(n, bank):
            src = normed[n % 2]
            pe.wait(normed_there[n], ident_there)
            pe.wait(*bank.readers)
            nT_turned[n] = run(pe, [lambda e, t=t: e.transpose(bank.ap[:, t * TILE:(t + 1) * TILE], src.ap[:, t, :], ident[:, :])
                                    for t in range(TILES)], nT_done)
            src.readers = [nT_turned[n]]

        nT_there = {}

        def norm_split(n, bank):
            hi, lo = nT_hi[n % 2], nT_lo[n % 2]
            act_q.wait(*hi.readers)
            dve.wait(*lo.readers)
            nT_there[n] = split(act_q, dve, [nT_turned[n]], bank.ap, hi.ap, lo.ap, nT_hi_made, nT_lo_made)
            bank.readers = [nT_there[n][1]]

        nT_bank, q_bank, k_bank, v_bank, s_bank, dT_bank, at_bank = banks[:7]
        ctx_split, q_there, k_there, v_there, exp_there = {}, {}, {}, {}, {}
        scale_there, diag_there, diagT_there, rows_there = {}, {}, {}, {}

        def split_ctx(g):
            hi, lo, src = ctx_hi[g % 2], ctx_lo[g % 2], ctx_in[g % 3]
            act_q.wait(*hi.readers)
            pool.wait(*lo.readers)
            ctx_split[g] = split(act_q, pool, [ctx_there[g]], src.ap, hi.ap, lo.ap, ctx_hi_made, ctx_lo_made)
            src.readers = [ctx_split[g][1]]

        def project_kv(g):
            hi, lo = ctx_hi[g % 2], ctx_lo[g % 2]
            pe.wait(*qkv_split, *ctx_split[g])
            pe.wait(*k_bank.readers)
            w = (qkv_hi[:, DIM:2 * DIM], qkv_lo[:, DIM:2 * DIM])
            k_ready = run(pe, passes(w, (hi.ap, lo.ap), k_bank.ap), k_done)
            pe.wait(*v_bank.readers)
            w = (qkv_hi[:, 2 * DIM:], qkv_lo[:, 2 * DIM:])
            steps = []
            for t in range(TILES):
                at = slice(t * TILE, (t + 1) * TILE)
                steps += passes((hi.ap[:, at], lo.ap[:, at]), w, v_bank.ap[:, t * DIM:(t + 1) * DIM])
            v_ready = run(pe, steps, v_done)
            hi.readers = lo.readers = [v_ready]
            k, v = kT[g % 2], vals[g % 3]
            act_q.wait(k_ready, small_there)
            act_q.wait(*k.readers)
            k_there[g] = act_q.make(k_made, lambda e: e.activation(k.ap, k_bank.ap, ACT.Identity, bias=bqk[:, 1:2]))
            k_bank.readers = [k_there[g]]
            dve.wait(v_ready, small_there)
            dve.wait(*v.readers)
            v_there[g] = dve.make(v_made, lambda e: e.tensor_tensor(
                v.ap, v_bank.ap.rearrange("p (t d) -> p t d", t=TILES),
                bv_all[:, :].unsqueeze(1).to_broadcast([P, TILES, DIM]), ALU.add))
            v_bank.readers = [v_there[g]]

        def project_q(g):
            hi, lo, q = nT_hi[g % 2], nT_lo[g % 2], qT[g % 2]
            pe.wait(*nT_there[g])
            pe.wait(*q_bank.readers)
            q_ready = run(pe, passes((qkv_hi[:, :DIM], qkv_lo[:, :DIM]), (hi.ap, lo.ap), q_bank.ap), q_done)
            hi.readers = lo.readers = [q_ready]
            act_q.wait(q_ready)
            act_q.wait(*q.readers)
            q_there[g] = act_q.make(q_made, lambda e: e.activation(q.ap, q_bank.ap, ACT.Identity, bias=bqk[:, 0:1]))
            q_bank.readers = [q_there[g]]

        max_there, scores_ready = {}, {}

        def make_scores(g):
            q, k = qT[g % 2], kT[g % 2]
            pe.wait(q_there[g], k_there[g])
            pe.wait(*s_bank.readers)
            steps = []
            for t in range(TILES):
                for b in range(PAIR):
                    at = slice(t * TILE + b * SEQ, t * TILE + (b + 1) * SEQ)
                    steps.append(lambda e, at=at, t=t, b=b: e.matmul(
                        s_bank.ap[b * SEQ:(b + 1) * SEQ, t * SEQ:(t + 1) * SEQ], q.ap[:, at], k.ap[:, at],
                        start=True, stop=True))
            scores_ready[g] = run(pe, steps, scores_done)
            q.readers = k.readers = [scores_ready[g]]

        def mask_scores(g):
            sc, mx = scores[g % 2], row_max[g % 2]
            kept = keep[:, TILES * g:TILES * (g + 1), :]
            pool.wait(*sc.readers)
            filled = pool.make(fill_made, lambda e: e.memset(sc.ap, MASKED))
            dve.wait(mask_there)
            keep_there = dve.make(keep_made, lambda e: e.tensor_scalar(
                kept, mask_sb[:, TILES * g:TILES * (g + 1), :], 0.0, None, ALU.is_equal))
            dve.wait(scores_ready[g], filled, keep_there)
            made = dve.make(scores_made, lambda e: e.copy_predicated(
                sc.ap, kept, s_bank.ap[:, :TILES * SEQ].rearrange("p (t k) -> p t k", t=TILES)))
            s_bank.readers = [made]
            dve.wait(made)
            dve.wait(*mx.readers)
            max_there[g] = dve.make(max_made, lambda e: e.reduce_max(mx.ap, sc.ap, X))
            pool.wait(max_there[g])
            off = pool.make(shifted, lambda e: e.tensor_tensor(
                sc.ap, sc.ap, mx.ap.unsqueeze(2).to_broadcast([P, TILES, SEQ]), ALU.subtract))
            mx.readers = [off]
            pr = probs[g % 2]
            act_q.wait(off)
            act_q.wait(*pr.readers)
            exp_there[g] = act_q.make(exp_made, lambda e: e.activation(pr.ap, sc.ap, ACT.Exp, scale=SCALE))
            sc.readers = [exp_there[g]]

        def normalise(g):
            pr, sm, iv, rs, dg = probs[g % 2], row_sum[g % 2], row_inv[g % 2], row_scale[g % 2], diag[g % 2]
            dve.wait(exp_there[g])
            dve.wait(*iv.readers)
            summed = dve.make(sum_made, lambda e: e.reduce_sum(sm.ap, pr.ap, X))
            dve.wait(summed)
            inverted = dve.make(inv_made, lambda e: e.reciprocal(iv.ap, sm.ap))
            dve.wait(inverted, gate_own_there)
            dve.wait(*rs.readers)
            full = [P, TILES, PAIR]
            scale_there[g] = dve.make(scale_made, lambda e: e.tensor_tensor(
                rs.ap, iv.ap.unsqueeze(2).to_broadcast(full), gate_own[:, :].unsqueeze(1).to_broadcast(full), ALU.mult))
            iv.readers = [scale_there[g]]
            pool.wait(scale_there[g])
            pool.wait(*dg.readers)
            full4 = [P, TILES, PAIR, SEQ]
            diag_there[g] = pool.make(diag_made, lambda e: e.tensor_tensor(
                dg.ap.rearrange("p t (b k) -> p t b k", b=PAIR), pr.ap.unsqueeze(2).to_broadcast(full4),
                rs.ap.unsqueeze(3).to_broadcast(full4), ALU.mult))
            pr.readers = rs.readers = [diag_there[g]]

        def turn_probs(g):
            dg, dt = diag[g % 2], diagT[g % 2]
            pe.wait(diag_there[g])
            pe.wait(*dT_bank.readers)
            turned = run(pe, [lambda e, t=t: e.transpose(dT_bank.ap[:, t * TILE:(t + 1) * TILE], dg.ap[:, t, :], ident[:, :])
                              for t in range(TILES)], diagT_done)
            dg.readers = [turned]
            act_q.wait(turned)
            act_q.wait(*dt.readers)
            diagT_there[g] = act_q.make(diagT_made, lambda e: e.activation(
                dt.ap, dT_bank.ap.rearrange("p (t c) -> p t c", t=TILES), ACT.Copy))
            dT_bank.readers = [diagT_there[g]]

        def attend(g):
            dt, v = diagT[g % 2], vals[g % 3]
            pe.wait(diagT_there[g], v_there[g])
            pe.wait(*at_bank.readers)
            attended = run(pe, [lambda e, t=t: e.matmul(at_bank.ap[:, t * DIM:(t + 1) * DIM], dt.ap[:, t, :], v.ap[:, t, :],
                                                        start=True, stop=True) for t in range(TILES)], attn_done)
            dt.readers = v.readers = [attended]
            dve.wait(attended, normed_there[g])
            rows_there[g] = dve.make(rows_made, lambda e: e.tensor_tensor(
                row_of(g), row_of(g), at_bank.ap.rearrange("p (t d) -> p t d", t=TILES), ALU.add))
            at_bank.readers = [rows_there[g]]

        w_split = {}

        def split_weights(c):
            at = slice(c * GROUP, min((c + 1) * GROUP, WCOLS))
            w_split[c] = split(act_q, pool, [w_there], raw[:, at], w_hi[:, at], w_lo[:, at], w_split_hi, w_split_lo)

        for s in range(GROUPS + 3):
            now, last, before, oldest = s, s - 1, s - 2, s - 3
            has = lambda g: 0 <= g < GROUPS
            if s + 2 < GROUPS:
                load_x(s + 2)
                load_ctx(s + 2)
            if has(now):
                finish_chore(norm_stats(now, now, [x_there[now]]))
            if has(last):
                norm_turn(last, nT_bank)
                norm_split(last, nT_bank)
            if has(oldest):
                turn_probs(oldest)
            if has(before):
                make_scores(before)
                mask_scores(before)
            if has(now):
                finish_chore(norm_apply(now, now))
                split_ctx(now)
            if has(last):
                project_kv(last)
            if has(before):
                normalise(before)
            if has(last):
                project_q(last)
            if has(oldest):
                attend(oldest)
            if 1 <= s and (s - 1) * GROUP < WCOLS:
                split_weights(s - 1)

        up_banks, gate_banks, hT_banks, y_bank, side_bank = banks[0:2], banks[2:4], banks[4:6], banks[6], banks[7]
        all_weights = [m for pair in w_split.values() for m in pair]
        units = 0
        attention_over = [q_there[GROUPS - 1], scores_ready[GROUPS - 1], exp_there[GROUPS - 1], diag_there[GROUPS - 1],
                          diagT_there[GROUPS - 1], rows_there[GROUPS - 1]] + all_weights
        th_there, sh_act_there, s1_there, s2_there, sh_hid_there = {}, {}, {}, {}, {}
        hid_count = 0

        def shared_layer1(g, pair):
            nonlocal units
            n = GROUPS + g
            hi, lo = nT_hi[n % 2], nT_lo[n % 2]
            u = units
            units += 1
            pe.wait(*nT_there[n], *all_weights)
            ac, hd = act[act_turn(g, pair)], sh_hid[g % 2]
            for i in range(2):
                t = 2 * pair + i
                bank = (up_banks, gate_banks)[i][u % 2]
                at = slice(t * TILE, (t + 1) * TILE)
                out_ap = bank.ap[:, :SHARED_COLS]
                pe.wait(*bank.readers)
                w = slice(WSH, WSH + SHARED_COLS)
                ready = run(pe, passes((hi.ap[:, at], lo.ap[:, at]), (w_hi[:, w], w_lo[:, w]), out_ap), sh_done)
                act_q.wait(ready)
                act_q.wait(*ac.readers)
                if t == 0:
                    act_q.wait(*th[g % 2].readers)
                th_there[g] = act_q.make(th_made, lambda e, bank=bank, t=t: e.activation(
                    th[g % 2].ap[:, t, :], bank.ap[:, 2 * DIM:SHARED_COLS], ACT.Tanh, scale=0.5))
                silu = act_q.make(sh_act_made, lambda e, bank=bank, i=i: e.activation(
                    ac.ap[:, i, :], bank.ap[:, :DIM], ACT.Silu))
                dve.wait(silu)
                if t == 0:
                    dve.wait(*hd.readers)
                sh_hid_there[g] = dve.make(sh_hid_made, lambda e, bank=bank, i=i, t=t: e.tensor_tensor(
                    hd.ap[:, t, :], ac.ap[:, i, :], bank.ap[:, DIM:2 * DIM], ALU.mult))
                bank.readers = [sh_hid_there[g]]
            ac.readers = [sh_hid_there[g]]

        turns = 0

        def act_turn(*_):
            nonlocal turns
            turns += 1
            return (turns - 1) % 3

        def route(g):
            i = g % 2
            dve.wait(th_there[g])
            dve.wait(*sig[i].readers)
            a = dve.make(sig_made, lambda e: e.tensor_scalar(sig[i].ap, th[i].ap, 0.5, 0.5, ALU.mult, ALU.add))
            th[i].readers = [a]
            yield
            dve.wait(a, small_there)
            b = dve.make(ranked_made, lambda e: e.tensor_tensor(
                ranked[i].ap, sig[i].ap, bias_all[:, :].unsqueeze(1).to_broadcast([P, TILES, EXPERTS]), ALU.add))
            yield
            dve.wait(b)
            full = [P, TILES, EXPERTS, EXPERTS]
            other, own = ranked[i].ap.unsqueeze(2).to_broadcast(full), ranked[i].ap.unsqueeze(3).to_broadcast(full)
            dve.wait(*over[i].readers)
            c = dve.make(over_made, lambda e: e.tensor_tensor(over[i].ap, other, own, ALU.is_gt))
            d = dve.make(least_made, lambda e: e.tensor_tensor(least[i].ap, other, own, ALU.is_ge))
            yield
            pool.wait(c, d, tri_there)
            f = pool.make(tie_made, lambda e: e.tensor_tensor(over[i].ap, over[i].ap, upper[:, :, :, :], ALU.mult))
            h = pool.make(tie_made, lambda e: e.tensor_tensor(least[i].ap, least[i].ap, lower[:, :, :, :], ALU.mult))
            pool.wait(f, h)
            k = pool.make(tie_made, lambda e: e.tensor_tensor(over[i].ap, over[i].ap, least[i].ap, ALU.add))
            yield
            yield
            dve.wait(k)
            r = dve.make(rank_made, lambda e: e.reduce_sum(rank[i].ap, over[i].ap, X))
            over[i].readers = [r]
            yield
            dve.wait(r)
            ch = dve.make(chosen_made, lambda e: e.tensor_scalar(chosen[i].ap, rank[i].ap, float(TOP_K), None, ALU.is_lt))
            yield
            dve.wait(ch)
            dve.wait(*s1[i].readers)
            s1_there[g] = dve.make(s1_made, lambda e: e.tensor_tensor(s1[i].ap, chosen[i].ap, sig[i].ap, ALU.mult))
            sig[i].readers = [s1_there[g]]
            yield
            dve.wait(s1_there[g])
            dve.wait(*s2[i].readers)
            s2_there[g] = dve.make(s2_made, lambda e: e.tensor_tensor(s2[i].ap, s1[i].ap, s1[i].ap, ALU.mult))
            yield

        hid_there = {}

        def layer1(g, u):
            nonlocal units, hid_count
            t, half = u // HALVES, u % HALVES
            n = GROUPS + g
            hi, lo = nT_hi[n % 2], nT_lo[n % 2]
            at = slice(t * TILE, (t + 1) * TILE)
            up, gt = up_banks[units % 2], gate_banks[units % 2]
            units += 1
            pe.wait(*nT_there[n], *all_weights)
            ready = []
            for m, (bank, made) in enumerate(((up, up_done), (gt, gate_done))):
                c = W13 + (half * 2 + m) * PER_HALF * DIM
                w = slice(c, c + PER_HALF * DIM)
                pe.wait(*bank.readers)
                ready.append(run(pe, passes((hi.ap[:, at], lo.ap[:, at]), (w_hi[:, w], w_lo[:, w]), bank.ap), made))
            if u == TILES * HALVES - 1:
                hi.readers = lo.readers = [ready[1]]
            ac, hd = act[act_turn()], hid[hid_count % 4]
            hid_count += 1
            act_q.wait(ready[0], s1_there[g])
            act_q.wait(*ac.readers)
            for j in range(PER_HALF):
                e_ = half * PER_HALF + j
                silu = act_q.make(act_made, lambda e, j=j, e_=e_: e.activation(
                    ac.ap[:, j, :], up.ap[:, j * DIM:(j + 1) * DIM], ACT.Silu, scale=s1[g % 2].ap[:, t, e_:e_ + 1]))
            up.readers = [silu]
            s1[g % 2].readers = [silu]
            dve.wait(silu, ready[1])
            dve.wait(*hd.readers)
            prod = dve.make(prod_made, lambda e: e.tensor_tensor(
                hd.ap, ac.ap, gt.ap.rearrange("p (j d) -> p j d", j=PER_HALF), ALU.mult))
            ac.readers = gt.readers = [prod]
            drip()
            pool.wait(prod, s2_there[g])
            es = slice(half * PER_HALF, (half + 1) * PER_HALF)
            hid_there[g, u] = pool.make(hid_made, lambda e: e.tensor_tensor(
                hd.ap, hd.ap, s2[g % 2].ap[:, t, es].unsqueeze(2).to_broadcast([P, PER_HALF, DIM]), ALU.mult))
            s2[g % 2].readers = [hid_there[g, u]]
            waiting.append((hd, hid_there[g, u], slice(half * PER_HALF, (half + 1) * PER_HALF), at, g, u))

        waiting, turned_count = [], 0
        hT_there = {}
        y_ready = {}

        def turn_hidden():
            nonlocal turned_count
            hd, there, slots, at, g, unit = waiting.pop(0)
            bank = hT_banks[turned_count % 2]
            turned_count += 1
            pe.wait(there)
            pe.wait(*bank.readers)
            turned = run(pe, [lambda e, j=j: e.transpose(bank.ap[:, j * TILE:(j + 1) * TILE], hd.ap[:, j, :], ident[:, :])
                              for j in range(4)], hT_done)
            hd.readers = [turned]
            hi, lo, src = hT_hi[g % 2], hT_lo[g % 2], bank.ap
            if at is None:
                hi_ap, lo_ap = hi.ap[:, slots, :], lo.ap[:, slots, :]
            else:
                hi_ap, lo_ap, src = hi.ap[:, slots, at], lo.ap[:, slots, at], src.rearrange("p (j c) -> p j c", j=PER_HALF)
            act_q.wait(*attention_over, *hi.readers)
            dve.wait(*attention_over, *lo.readers)
            pair = split(act_q, dve, [turned], src, hi_ap, lo_ap, hT_hi_made, hT_lo_made)
            bank.readers = [pair[1]]
            hT_there[g, unit] = pair
            drip()

        yT_there = {}

        def layer2(g, piece):
            order = ([SHARED] + list(range(EXPERTS)))[2 * piece:2 * piece + 2]
            if piece == 0:
                pe.wait(*y_bank.readers)
            hi, lo = hT_hi[g % 2], hT_lo[g % 2]
            steps = []
            for e_ in order:
                last_unit = SHARED if e_ == SHARED else (TILES - 1) * HALVES + e_ // PER_HALF
                pe.wait(*hT_there[g, last_unit])
                c = WSH2 if e_ == SHARED else W2 + e_ * DIM
                w = slice(c, c + DIM)
                steps = passes((w_hi[:, w], w_lo[:, w]), (hi.ap[:, e_, :], lo.ap[:, e_, :]), y_bank.ap,
                               first=(e_ == SHARED), last=(e_ == EXPERTS - 1))
                done = run(pe, steps, y_done)
            if order[-1] != EXPERTS - 1:
                return
            hi.readers = lo.readers = [done]
            act_q.wait(done, tanh_there)
            act_q.wait(*y_sb[0].readers)
            yT_there[g] = act_q.make(y_made, lambda e: e.activation(y_sb[0].ap, y_bank.ap, ACT.Copy, scale=gate_t[:, 1:2]))
            y_bank.readers = [yT_there[g]]

        def finish(g):
            pe.wait(yT_there[g])
            pe.wait(*side_bank.readers)
            turned = run(pe, [lambda e, t=t: e.transpose(side_bank.ap[:, t * DIM:(t + 1) * DIM],
                                                         y_sb[0].ap[:, t * TILE:(t + 1) * TILE], ident[:, :])
                              for t in range(TILES)], yT_done)
            y_sb[0].readers = [turned]
            dve.wait(turned, normed_there[GROUPS + g])
            made = dve.make(result_made, lambda e: e.tensor_tensor(
                row_of(g), row_of(g), side_bank.ap.rearrange("p (t d) -> p t d", t=TILES), ALU.add))
            side_bank.readers = [made]
            sp.wait(made)
            return sp.make(stored, lambda e: e.dma_start(out_tiles[:, TILES * g:TILES * (g + 1), :], row_of(g)), 16)

        def prepare(g, part):
            if g >= GROUPS:
                return
            n = GROUPS + g
            if part == 0:
                chores.append(norm_stats(n, g, [rows_there[g]]))
                chores.append(norm_apply(n, g))
            elif part == 1:
                norm_turn(n, side_bank)
                norm_split(n, side_bank)
            elif part == 2:
                shared_layer1(g, 0)
            elif part == 3:
                shared_layer1(g, 1)
                chores.append(route(g))
                waiting.append((sh_hid[g % 2], sh_hid_there[g], SHARED, None, g, SHARED))

        def drain_chores():
            while chores:
                finish_chore(chores.pop(0))

        for part in range(4):
            prepare(0, part)
            drain_chores()
        PREPARE_AT = {0: 0, 2: 1, 3: 2, 4: 3}
        LAYER2_AT = {1: [0], 2: [1], 3: [2], 4: [3], 5: [4]}
        FINISH_AT = 6
        for g in range(GROUPS):
            for u in range(TILES * HALVES):
                layer1(g, u)
                if g:
                    for piece in LAYER2_AT.get(u, []):
                        layer2(g - 1, piece)
                    if u == FINISH_AT:
                        finish(g - 1)
                if u in PREPARE_AT:
                    if PREPARE_AT[u]:
                        drain_chores()
                    prepare(g + 1, PREPARE_AT[u])
                while len(waiting) > 2:
                    turn_hidden()
            drain_chores()
        while waiting:
            turn_hidden()
        for piece in range(5):
            layer2(GROUPS - 1, piece)
        all_stored = finish(GROUPS - 1)
        sp.wait(all_stored)

        block = stack.enter_context(nc.Block())
        block.sync(sp.play)
        block.tensor(pe.play)
        block.vector(dve.play)
        block.scalar(act_q.play)
        block.gpsimd(pool.play)


def kernel(**inputs):
    import concourse.bacc as bacc
    from concourse.bass_utils import run_bass_kernel_spmd

    a = {k: np.asarray(v) for k, v in inputs.items()}
    down = lambda w: w.transpose(2, 0, 1)
    w1, w3 = (down(a[f"L0_ffn_w{i}"]).reshape(DIM, HALVES, PER_HALF * DIM) for i in (1, 3))
    w13 = np.stack([w1, w3], axis=2).reshape(DIM, -1)
    w_moe = np.concatenate([w13, down(a["L0_ffn_w2"]).reshape(DIM, -1), a["L0_ffn_sw1"].T, a["L0_ffn_sw3"].T,
                            a["L0_ffn_gate_w"].T, a["L0_ffn_sw2"].T], axis=1)
    arrays = {
        "x": a["x"].reshape(TOKENS, DIM),
        "ctx_t": a["ctx_1024"].reshape(TOKENS, DIM).T,
        "mask": a["mask_BxSxS2_bk1"].reshape(TOKENS // TILE, TILE, SEQ).transpose(1, 0, 2),
        "w_qkv": np.concatenate([a[f"L0_xattn_W{n}"].T for n in "qkv"], axis=1),
        "b_qk": np.stack([a["L0_xattn_bq"], a["L0_xattn_bk"]], axis=1),
        "bv_row": a["L0_xattn_bv"].reshape(1, DIM),
        "bias_row": a["L0_ffn_expert_bias"].reshape(1, EXPERTS),
        "gates": np.stack([a["g_xattn"], a["g_ffn"]], axis=1),
        "w_moe": w_moe,
    }
    arrays = {k: np.ascontiguousarray(v) for k, v in arrays.items()}
    nc = bacc.Bacc("TRN2", target_bir_lowering=False, num_devices=1)
    aps = [nc.dram_tensor(k, v.shape, mybir.dt.from_np(v.dtype), kind="ExternalInput").ap() for k, v in arrays.items()]
    out = nc.dram_tensor("out", (TOKENS, DIM), F32, kind="ExternalOutput").ap()
    build(nc, *aps, out)
    r = run_bass_kernel_spmd(nc, [arrays], core_ids=[0])
    return r.results[0]["out"].reshape(BATCHES, SEQ, DIM)
```

```python
from contextlib import ExitStack

import numpy as np

import concourse.bass as bass
from concourse import mybir

F32 = mybir.dt.float32
F32R = mybir.dt.float32r
U8 = mybir.dt.uint8
ALU = mybir.AluOpType
ACT = mybir.ActivationFunctionType
X = mybir.AxisListType.X

P = 128
BATCHES, SEQ, DIM = 128, 64, 128
EXPERTS, TOP_K = 8, 2
TOKENS = BATCHES * SEQ
TILE = P
TILES = 4
GROUP = TILES * TILE
GROUPS = TOKENS // GROUP
PAIR = TILE // SEQ
HALVES = 2
PER_HALF = EXPERTS // HALVES
SHARED = EXPERTS
SHARED_COLS = 2 * DIM + EXPERTS
EPS = 1e-5
SCALE = float(np.float32(1.0) / np.sqrt(np.float32(DIM)))
MASKED = -1e9 / SCALE

W13 = 0
W2 = W13 + 2 * EXPERTS * DIM
WSH = W2 + EXPERTS * DIM
WSH2 = WSH + SHARED_COLS
WCOLS = WSH2 + DIM


class Queue:

    def __init__(self):
        self.steps = []
        self.seen = {}

    def wait(self, *marks):
        for sem, value in marks:
            if self.seen.get(id(sem), 0) < value:
                self.seen[id(sem)] = value
                self.steps.append(lambda eng, s=sem, v=value: eng.wait_ge(s.handle, v))

    def do(self, instruction):
        self.steps.append(instruction)

    def make(self, sem, instruction, by=1):
        sem.value += by
        self.steps.append(lambda eng: instruction(eng).then_inc(sem.handle, by))
        return (sem, sem.value)

    def play(self, eng):
        for step in self.steps:
            step(eng)


class Counter:

    def __init__(self, handle):
        self.handle = handle
        self.value = 0


class Slot:

    def __init__(self, ap):
        self.ap = ap
        self.readers = []


def build(nc, x, ctx_t, mask, w_qkv, b_qk, bv_row, bias_row, gates, w_moe, out):
    stack = ExitStack()
    with stack:
        def sb(name, shape, dt=F32, scope=stack):
            return scope.enter_context(nc.sbuf_tensor(name, shape, dt))

        def sem(name):
            return Counter(stack.enter_context(nc.semaphore(name)))

        def ring(name, n, shape, dt=F32, scope=stack):
            whole = sb(name, [P, n] + shape, dt, scope)
            return [Slot(whole[:, i]) for i in range(n)]

        rows = sb("rows", [P, GROUPS * TILES, DIM])
        normed = ring("normed", 2, [TILES, DIM])
        nT_hi, nT_lo = ring("nT_hi", 2, [GROUP], F32R), ring("nT_lo", 2, [GROUP], F32R)
        y_sb = ring("y_sb", 1, [GROUP])
        act = ring("act", 3, [PER_HALF, DIM])
        hid = ring("hid", 4, [PER_HALF, DIM])
        w_hi, w_lo = sb("w_hi", [P, WCOLS], F32R), sb("w_lo", [P, WCOLS], F32R)
        bqk = sb("bqk", [P, 2])
        bv_all = sb("bv_all", [P, DIM])
        bias_all = sb("bias_all", [P, EXPERTS])
        gate_in, gate_t = sb("gate_in", [P, 2]), sb("gate_t", [P, 2])
        ident = sb("ident", [P, P])
        lower, upper = sb("lower", [P, TILES, EXPERTS, EXPERTS]), sb("upper", [P, TILES, EXPERTS, EXPERTS])
        own_half, gate_own = sb("own_half", [P, PAIR]), sb("gate_own", [P, PAIR])
        neg_half = sb("neg_half", [P, TILES])
        stats = ring("stats", 2, [TILES, 6])
        moments = ring("moments", 2, [TILES, 2])
        var_eps, rstd = ring("var_eps", 2, [TILES]), ring("rstd", 2, [TILES])
        row_max, row_sum, row_inv = ring("row_max", 2, [TILES]), ring("row_sum", 2, [TILES]), ring("row_inv", 2, [TILES])
        row_scale = ring("row_scale", 2, [TILES, PAIR])
        th = ring("th", 2, [TILES, EXPERTS])
        sig = ring("sig", 2, [TILES, EXPERTS])
        ranked = ring("ranked", 2, [TILES, EXPERTS])
        over, least = ring("over", 2, [TILES, EXPERTS, EXPERTS]), ring("least", 2, [TILES, EXPERTS, EXPERTS])
        rank, chosen = ring("rank", 2, [TILES, EXPERTS]), ring("chosen", 2, [TILES, EXPERTS])
        s1, s2 = ring("s1", 2, [TILES, EXPERTS]), ring("s2", 2, [TILES, EXPERTS])
        sh_hid = ring("sh_hid", 2, [TILES, DIM])
        attention = stack.enter_context(ExitStack())
        ctx_in = ring("ctx_in", 4, [GROUP], scope=attention)
        ctx_hi, ctx_lo = ring("ctx_hi", 2, [GROUP], F32R, scope=attention), ring("ctx_lo", 2, [GROUP], F32R, scope=attention)
        nT = ring("nT", 2, [GROUP], scope=attention)
        qT, kT = ring("qT", 2, [GROUP], scope=attention), ring("kT", 2, [GROUP], scope=attention)
        vals = ring("vals", 3, [TILES, DIM], scope=attention)
        scores = ring("scores", 2, [TILES, SEQ], scope=attention)
        probs = ring("probs", 2, [TILES, SEQ], scope=attention)
        diag = ring("diag", 2, [TILES, TILE], scope=attention)
        diagT = ring("diagT", 2, [TILES, TILE], scope=attention)
        raw = sb("raw", [P, WCOLS], scope=attention)
        qkv_raw = sb("qkv_raw", [P, 3 * DIM], scope=attention)
        wk_hi, wk_lo = sb("wk_hi", [P, DIM], F32R, scope=attention), sb("wk_lo", [P, DIM], F32R, scope=attention)
        mask_sb = sb("mask_sb", [P, GROUPS * TILES, SEQ], U8, scope=attention)
        masked = sb("masked", [P, TILES, SEQ], scope=attention)
        attention.close()
        hT_hi, hT_lo = ring("hT_hi", 2, [EXPERTS + 1, GROUP], F32R), ring("hT_lo", 2, [EXPERTS + 1, GROUP], F32R)
        banks = [Slot(stack.enter_context(nc.psum_tensor(f"bank{i}", [P, GROUP], F32))[:, :]) for i in range(8)]

        x_in = [sem(f"x_in{g}") for g in range(GROUPS)]
        ctx_come = [sem(f"ctx_come{i}") for i in range(4)]
        small_in, mask_in, w_in, qkv_in, gates_in = (sem(n) for n in ("small_in", "mask_in", "w_in", "qkv_in", "gates_in"))
        ident_made, tri_made, half_made, own_made, fill_made = (
            sem(n) for n in ("ident_made", "tri_made", "half_made", "own_made", "fill_made"))
        copied_made, tanh_g, gate_own_made, wk_split_hi, wk_split_lo, w_split_hi, w_split_lo = (
            sem(n) for n in ("copied_made", "tanh_g", "gate_own_made", "wk_split_hi", "wk_split_lo", "w_split_hi", "w_split_lo"))
        stats_made, moments_made, eps_added, rstd_made, normed_made = (
            sem(n) for n in ("stats_made", "moments_made", "eps_added", "rstd_made", "normed_made"))
        ctx_hi_made, ctx_lo_made, nT_made = sem("ctx_hi_made"), sem("ctx_lo_made"), sem("nT_made")
        nT_done, nT_hi_made, nT_lo_made = sem("nT_done"), sem("nT_hi_made"), sem("nT_lo_made")
        k_done, v_done, q_done = sem("k_done"), sem("v_done"), sem("q_done")
        k_made, v_made, q_made = sem("k_made"), sem("v_made"), sem("q_made")
        scores_done, scores_made, max_made, shifted, exp_made = (
            sem(n) for n in ("scores_done", "scores_made", "max_made", "shifted", "exp_made"))
        sum_made, inv_made, scale_made, diag_made = (sem(n) for n in ("sum_made", "inv_made", "scale_made", "diag_made"))
        diagT_done, diagT_made, attn_done, rows_made = (
            sem(n) for n in ("diagT_done", "diagT_made", "attn_done", "rows_made"))
        up_done, gate_done, act_made, prod_made, hid_made = (
            sem(n) for n in ("up_done", "gate_done", "act_made", "prod_made", "hid_made"))
        sh_done, sh_act_made, th_made, sh_hid_made = (sem(n) for n in ("sh_done", "sh_act_made", "th_made", "sh_hid_made"))
        sig_made, ranked_made, over_made, least_made, tie_made, rank_made, chosen_made, s1_made, s2_made = (
            sem(n) for n in ("sig_made", "ranked_made", "over_made", "least_made", "tie_made", "rank_made",
                             "chosen_made", "s1_made", "s2_made"))
        hT_done, hT_hi_made, hT_lo_made = sem("hT_done"), sem("hT_hi_made"), sem("hT_lo_made")
        y_done, y_made, yT_done, result_made = sem("y_done"), sem("y_made"), sem("yT_done"), sem("result_made")
        stored = sem("stored")

        sp, pe, dve, act_q, pool = Queue(), Queue(), Queue(), Queue(), Queue()

        row_of = lambda g: rows[:, TILES * g:TILES * (g + 1), :]
        x_tiles = x.rearrange("(t p) d -> p t d", p=P)
        out_tiles = out.rearrange("(t p) d -> p t d", p=P)
        x_there, ctx_there = {}, {}

        def load_x(g):
            x_there[g] = sp.make(x_in[g], lambda e: e.dma_start(row_of(g), x_tiles[:, TILES * g:TILES * (g + 1), :]), 16)

        def load_ctx(g):
            slot = ctx_in[g % 4]
            sp.wait(*slot.readers)
            ctx_there[g] = sp.make(ctx_come[g % 4], lambda e: e.dma_start(slot.ap, ctx_t[:, g * GROUP:(g + 1) * GROUP]), 16)

        load_x(0)
        load_ctx(0)
        qkv_there = sp.make(qkv_in, lambda e: e.dma_start(qkv_raw[:, :], w_qkv), 16)
        sp.make(small_in, lambda e: e.dma_start(bqk[:, :], b_qk), 16)
        sp.make(small_in, lambda e: e.dma_start(bv_all[:, :], bv_row.to_broadcast([P, DIM])), 16)
        small_there = sp.make(small_in, lambda e: e.dma_start(bias_all[:, :], bias_row.to_broadcast([P, EXPERTS])), 16)
        gates_there = sp.make(gates_in, lambda e: e.dma_start(gate_in[:, :], gates.to_broadcast([P, 2])), 16)
        load_x(1)
        load_ctx(1)
        mask_there = sp.make(mask_in, lambda e: e.dma_start(mask_sb[:, :, :], mask), 16)
        w_there = sp.make(w_in, lambda e: e.dma_start(raw[:, :], w_moe), 16)

        zeroed = pool.make(ident_made, lambda e: e.memset(ident[:, :], 0.0))
        pool.wait(zeroed)
        ident_there = pool.make(ident_made, lambda e: e.affine_select(
            out=ident[:, :], in_=ident[:, :], compare_op=ALU.not_equal, fill=1.0, base=0, pattern=[[-1, P]],
            channel_multiplier=1))
        half_there = pool.make(half_made, lambda e: e.memset(neg_half[:, :], -0.5))
        half_ones = pool.make(own_made, lambda e: e.memset(own_half[:, :], 1.0))
        pool.wait(half_ones)
        for b, (base, step) in enumerate(((SEQ - 1, -1), (-SEQ, 1))):
            own_there = pool.make(own_made, lambda e, b=b, base=base, step=step: e.affine_select(
                out=own_half[:, b:b + 1], in_=own_half[:, b:b + 1], compare_op=ALU.is_ge, fill=0.0, base=base,
                pattern=[[0, 1]], channel_multiplier=step))
        fill_there = pool.make(fill_made, lambda e: e.memset(masked[:, :, :], MASKED))
        tri_made_ones = [pool.make(tri_made, lambda e, t=t: e.memset(t[:, :, :, :], 1.0)) for t in (lower, upper)]
        pool.wait(*tri_made_ones)
        for t, sign in ((lower, 1), (upper, -1)):
            tri_there = pool.make(tri_made, lambda e, t=t, sign=sign: e.affine_select(
                out=t[:, :, :, :], in_=t[:, :, :, :], compare_op=ALU.is_gt, fill=0.0, base=0,
                pattern=[[0, TILES], [sign, EXPERTS], [-sign, EXPERTS]], channel_multiplier=0))
        act_q.wait(gates_there)
        tanh_there = act_q.make(tanh_g, lambda e: e.activation(gate_t[:, :], gate_in[:, :], ACT.Tanh))

        def split(hi_queue, lo_queue, there, src, hi, lo, hi_sem, lo_sem):
            hi_queue.wait(*there)
            if hi_queue is act_q:
                hi_there = hi_queue.make(hi_sem, lambda e: e.activation(hi, src, ACT.Copy))
            else:
                hi_there = hi_queue.make(hi_sem, lambda e: e.tensor_copy(hi, src))
            lo_queue.wait(hi_there)
            lo_there = lo_queue.make(lo_sem, lambda e: e.tensor_tensor(lo, src, hi.bitcast(F32), ALU.subtract))
            return hi_there, lo_there

        def passes(w_pair, m_pair, out_ap, first=True, last=True):
            order = ((w_pair[0], m_pair[0]), (w_pair[0], m_pair[1]), (w_pair[1], m_pair[0]))
            return [lambda e, w=w, m=m, a=(first and n == 0), b=(last and n == 2): e.matmul(out_ap, w, m, start=a, stop=b)
                    for n, (w, m) in enumerate(order)]

        def run(queue, instructions, sem_=None):
            for ins in instructions[:-1]:
                queue.do(ins)
            if sem_ is None:
                queue.do(instructions[-1])
                return None
            return queue.make(sem_, instructions[-1])

        chores = []

        def finish_chore(chore):
            for _ in chore:
                pass

        def drip():
            if chores:
                try:
                    next(chores[0])
                except StopIteration:
                    chores.pop(0)
                    drip()

        def drain_chores():
            while chores:
                finish_chore(chores.pop(0))

        rstd_there, moments_there, normed_there = {}, {}, {}

        def norm_stats(n, g, rows_there):
            st, mo, ve, rs = (r[n % 2] for r in (stats, moments, var_eps, rstd))
            dve.wait(*rows_there)
            src = row_of(g)
            for t in range(TILES):
                if t == 2:
                    yield
                made = dve.make(stats_made, lambda e, t=t: e.bn_stats(st.ap[:, t, :], src[:, t, :]))
            yield
            dve.wait(made)
            dve.wait(*mo.readers)
            for t in range(TILES):
                moments_there[n] = dve.make(moments_made, lambda e, t=t: e.bn_aggr(mo.ap[:, t, :], st.ap[:, t, :]))
            pool.wait(moments_there[n], half_there)
            pool.wait(*rs.readers)
            eps_there = pool.make(eps_added, lambda e: e.tensor_scalar(ve.ap, mo.ap[:, :, 1], EPS, None, ALU.add))
            pool.wait(eps_there)
            rstd_there[n] = pool.make(rstd_made, lambda e: e.tensor_tensor(rs.ap, ve.ap, neg_half[:, :], ALU.pow))
            yield
            yield
            yield

        def norm_apply(n, g):
            dst, mo, rs = normed[n % 2], moments[n % 2], rstd[n % 2]
            dve.wait(rstd_there[n])
            dve.wait(*dst.readers)
            src = row_of(g)
            for t in range(TILES):
                if t == 2:
                    yield
                normed_there[n] = dve.make(normed_made, lambda e, t=t: e.tensor_scalar(
                    dst.ap[:, t, :], src[:, t, :], mo.ap[:, t, 0:1], rs.ap[:, t:t + 1], ALU.subtract, ALU.mult))
            mo.readers = rs.readers = [normed_there[n]]
            yield

        nT_turned = {}

        def norm_turn(n, bank):
            src = normed[n % 2]
            pe.wait(normed_there[n], ident_there)
            pe.wait(*bank.readers)
            nT_turned[n] = run(pe, [lambda e, t=t: e.transpose(bank.ap[:, t * TILE:(t + 1) * TILE], src.ap[:, t, :], ident[:, :])
                                    for t in range(TILES)], nT_done)
            src.readers = [nT_turned[n]]

        nT_there = {}

        def norm_split(n, bank):
            hi, lo = nT_hi[n % 2], nT_lo[n % 2]
            act_q.wait(*hi.readers)
            dve.wait(*lo.readers)
            nT_there[n] = split(act_q, dve, [nT_turned[n]], bank.ap, hi.ap, lo.ap, nT_hi_made, nT_lo_made)
            bank.readers = [nT_there[n][1]]

        nT_bank, q_bank, k_bank, v_bank, s_bank, dT_bank, at_bank = banks[:7]
        ctx_split, q_there, k_there, v_there, exp_there = {}, {}, {}, {}, {}
        scale_there, diag_there, diagT_there, rows_there = {}, {}, {}, {}

        def split_ctx(g):
            hi, lo, src = ctx_hi[g % 2], ctx_lo[g % 2], ctx_in[g % 4]
            act_q.wait(*hi.readers)
            pool.wait(*lo.readers)
            ctx_split[g] = split(act_q, pool, [ctx_there[g]], src.ap, hi.ap, lo.ap, ctx_hi_made, ctx_lo_made)
            src.readers = [ctx_split[g][1]]

        def project_kv(g):
            hi, lo = ctx_hi[g % 2], ctx_lo[g % 2]
            pe.wait(*wk_split, *ctx_split[g], ctx_there[g], qkv_there)
            pe.wait(*k_bank.readers)
            w = (wk_hi[:, :], wk_lo[:, :])
            k_ready = run(pe, passes(w, (hi.ap, lo.ap), k_bank.ap), k_done)
            pe.wait(*v_bank.readers)
            hi.readers = lo.readers = [k_ready]
            src = ctx_in[g % 4]
            v_ready = run(pe, [lambda e, t=t: e.matmul(
                v_bank.ap[:, t * DIM:(t + 1) * DIM], src.ap[:, t * TILE:(t + 1) * TILE], qkv_raw[:, 2 * DIM:],
                start=True, stop=True) for t in range(TILES)], v_done)
            src.readers = src.readers + [v_ready]
            k, v = kT[g % 2], vals[g % 3]
            act_q.wait(k_ready, small_there)
            act_q.wait(*k.readers)
            k_there[g] = act_q.make(k_made, lambda e: e.activation(k.ap, k_bank.ap, ACT.Identity, bias=bqk[:, 1:2]))
            k_bank.readers = [k_there[g]]
            dve.wait(v_ready, small_there)
            dve.wait(*v.readers)
            v_there[g] = dve.make(v_made, lambda e: e.tensor_tensor(
                v.ap, v_bank.ap.rearrange("p (t d) -> p t d", t=TILES),
                bv_all[:, :].unsqueeze(1).to_broadcast([P, TILES, DIM]), ALU.add))
            v_bank.readers = [v_there[g]]

        nT_copied = {}

        def norm_copy(g, bank):
            dst = nT[g % 2]
            act_q.wait(nT_turned[g])
            act_q.wait(*dst.readers)
            nT_copied[g] = act_q.make(nT_made, lambda e: e.activation(dst.ap, bank.ap, ACT.Copy))
            bank.readers = [nT_copied[g]]

        def project_q(g):
            src, q = nT[g % 2], qT[g % 2]
            pe.wait(nT_copied[g], qkv_there)
            pe.wait(*q_bank.readers)
            q_ready = pe.make(q_done, lambda e: e.matmul(q_bank.ap, qkv_raw[:, :DIM], src.ap, start=True, stop=True))
            src.readers = [q_ready]
            act_q.wait(q_ready)
            act_q.wait(*q.readers)
            q_there[g] = act_q.make(q_made, lambda e: e.activation(q.ap, q_bank.ap, ACT.Identity, bias=bqk[:, 0:1]))
            q_bank.readers = [q_there[g]]

        max_there, scores_ready = {}, {}

        def make_scores(g):
            q, k = qT[g % 2], kT[g % 2]
            pe.wait(q_there[g], k_there[g])
            pe.wait(*s_bank.readers)
            steps = []
            for t in range(TILES):
                for b in range(PAIR):
                    at = slice(t * TILE + b * SEQ, t * TILE + (b + 1) * SEQ)
                    steps.append(lambda e, at=at, t=t, b=b: e.matmul(
                        s_bank.ap[b * SEQ:(b + 1) * SEQ, t * SEQ:(t + 1) * SEQ], q.ap[:, at], k.ap[:, at],
                        start=True, stop=True))
            scores_ready[g] = run(pe, steps, scores_done)
            q.readers = k.readers = [scores_ready[g]]

        shifted_there = {}

        def mask_scores(g):
            sc, mx = scores[g % 2], row_max[g % 2]
            act_q.wait(scores_ready[g])
            act_q.wait(*sc.readers)
            copied = act_q.make(copied_made, lambda e: e.activation(
                sc.ap, s_bank.ap[:, :TILES * SEQ].rearrange("p (t k) -> p t k", t=TILES), ACT.Copy))
            s_bank.readers = [copied]
            dve.wait(copied, mask_there, fill_there)
            made = dve.make(scores_made, lambda e: e.copy_predicated(
                sc.ap, mask_sb[:, TILES * g:TILES * (g + 1), :], masked[:, :, :]))
            dve.wait(made)
            dve.wait(*mx.readers)
            max_there[g] = dve.make(max_made, lambda e: e.reduce_max(mx.ap, sc.ap, X))
            pool.wait(max_there[g])
            off = pool.make(shifted, lambda e: e.tensor_tensor(
                sc.ap, sc.ap, mx.ap.unsqueeze(2).to_broadcast([P, TILES, SEQ]), ALU.subtract))
            mx.readers = [off]
            shifted_there[g] = off

        def exponents(g):
            sc, pr = scores[g % 2], probs[g % 2]
            act_q.wait(shifted_there[g])
            act_q.wait(*pr.readers)
            exp_there[g] = act_q.make(exp_made, lambda e: e.activation(pr.ap, sc.ap, ACT.Exp, scale=SCALE))
            sc.readers = [exp_there[g]]

        def normalise(g):
            pr, sm, iv, rs, dg = probs[g % 2], row_sum[g % 2], row_inv[g % 2], row_scale[g % 2], diag[g % 2]
            dve.wait(exp_there[g])
            dve.wait(*iv.readers)
            summed = dve.make(sum_made, lambda e: e.reduce_sum(sm.ap, pr.ap, X))
            yield
            dve.wait(summed)
            inverted = dve.make(inv_made, lambda e: e.reciprocal(iv.ap, sm.ap))
            yield
            dve.wait(inverted, gate_own_there)
            dve.wait(*rs.readers)
            full = [P, TILES, PAIR]
            scale_there[g] = dve.make(scale_made, lambda e: e.tensor_tensor(
                rs.ap, iv.ap.unsqueeze(2).to_broadcast(full), gate_own[:, :].unsqueeze(1).to_broadcast(full), ALU.mult))
            iv.readers = [scale_there[g]]
            pool.wait(scale_there[g])
            pool.wait(*dg.readers)
            full4 = [P, TILES, PAIR, SEQ]
            diag_there[g] = pool.make(diag_made, lambda e: e.tensor_tensor(
                dg.ap.rearrange("p t (b k) -> p t b k", b=PAIR), pr.ap.unsqueeze(2).to_broadcast(full4),
                rs.ap.unsqueeze(3).to_broadcast(full4), ALU.mult))
            pr.readers = rs.readers = [diag_there[g]]
            yield

        def turn_probs(g):
            dg, dt = diag[g % 2], diagT[g % 2]
            pe.wait(diag_there[g])
            pe.wait(*dT_bank.readers)
            turned = run(pe, [lambda e, t=t: e.transpose(dT_bank.ap[:, t * TILE:(t + 1) * TILE], dg.ap[:, t, :], ident[:, :])
                              for t in range(TILES)], diagT_done)
            dg.readers = [turned]
            act_q.wait(turned)
            act_q.wait(*dt.readers)
            diagT_there[g] = act_q.make(diagT_made, lambda e: e.activation(
                dt.ap, dT_bank.ap.rearrange("p (t c) -> p t c", t=TILES), ACT.Copy))
            dT_bank.readers = [diagT_there[g]]

        def attend(g):
            dt, v = diagT[g % 2], vals[g % 3]
            pe.wait(diagT_there[g], v_there[g])
            pe.wait(*at_bank.readers)
            attended = run(pe, [lambda e, t=t: e.matmul(at_bank.ap[:, t * DIM:(t + 1) * DIM], dt.ap[:, t, :], v.ap[:, t, :],
                                                        start=True, stop=True) for t in range(TILES)], attn_done)
            dt.readers = v.readers = [attended]
            dve.wait(attended, normed_there[g])
            rows_there[g] = dve.make(rows_made, lambda e: e.tensor_tensor(
                row_of(g), row_of(g), at_bank.ap.rearrange("p (t d) -> p t d", t=TILES), ALU.add))
            at_bank.readers = [rows_there[g]]

        w_split = {}
        W_CHUNK = GROUP // 2

        def split_weights(c):
            at = slice(c * W_CHUNK, min((c + 1) * W_CHUNK, WCOLS))
            w_split[c] = split(act_q, pool, [w_there], raw[:, at], w_hi[:, at], w_lo[:, at], w_split_hi, w_split_lo)

        up_banks, gate_banks, hT_banks, y_bank, side_bank = banks[0:2], banks[2:4], banks[4:6], banks[6], banks[7]
        all_weights, attention_over = [], []
        units = 0
        th_there, s1_there, s2_there, sh_hid_there = {}, {}, {}, {}
        hid_count = 0

        def shared_layer1(g, pair):
            nonlocal units
            n = GROUPS + g
            hi, lo = nT_hi[n % 2], nT_lo[n % 2]
            u = units
            units += 1
            pe.wait(*nT_there[n], *all_weights)
            ac, hd = act[act_turn()], sh_hid[g % 2]
            for i in range(2):
                t = 2 * pair + i
                bank = (up_banks, gate_banks)[i][u % 2]
                at = slice(t * TILE, (t + 1) * TILE)
                out_ap = bank.ap[:, :SHARED_COLS]
                pe.wait(*bank.readers)
                w = slice(WSH, WSH + SHARED_COLS)
                ready = run(pe, passes((hi.ap[:, at], lo.ap[:, at]), (w_hi[:, w], w_lo[:, w]), out_ap), sh_done)
                act_q.wait(ready)
                act_q.wait(*ac.readers)
                if t == 0:
                    act_q.wait(*th[g % 2].readers)
                th_there[g] = act_q.make(th_made, lambda e, bank=bank, t=t: e.activation(
                    th[g % 2].ap[:, t, :], bank.ap[:, 2 * DIM:SHARED_COLS], ACT.Tanh, scale=0.5))
                silu = act_q.make(sh_act_made, lambda e, bank=bank, i=i: e.activation(
                    ac.ap[:, i, :], bank.ap[:, :DIM], ACT.Silu))
                dve.wait(silu)
                if t == 0:
                    dve.wait(*hd.readers)
                sh_hid_there[g] = dve.make(sh_hid_made, lambda e, bank=bank, i=i, t=t: e.tensor_tensor(
                    hd.ap[:, t, :], ac.ap[:, i, :], bank.ap[:, DIM:2 * DIM], ALU.mult))
                bank.readers = [sh_hid_there[g]]
            ac.readers = [sh_hid_there[g]]

        turns = 0

        def act_turn():
            nonlocal turns
            turns += 1
            return (turns - 1) % len(act)

        def route(g, ties):
            i = g % 2
            dve.wait(th_there[g])
            dve.wait(*sig[i].readers)
            a = dve.make(sig_made, lambda e: e.tensor_scalar(sig[i].ap, th[i].ap, 0.5, 0.5, ALU.mult, ALU.add))
            th[i].readers = [a]
            yield
            dve.wait(a, small_there)
            b = dve.make(ranked_made, lambda e: e.tensor_tensor(
                ranked[i].ap, sig[i].ap, bias_all[:, :].unsqueeze(1).to_broadcast([P, TILES, EXPERTS]), ALU.add))
            yield
            dve.wait(b)
            full = [P, TILES, EXPERTS, EXPERTS]
            other, own = ranked[i].ap.unsqueeze(2).to_broadcast(full), ranked[i].ap.unsqueeze(3).to_broadcast(full)
            dve.wait(*over[i].readers)
            c = dve.make(over_made, lambda e: e.tensor_tensor(over[i].ap, other, own, ALU.is_gt))
            d = dve.make(least_made, lambda e: e.tensor_tensor(least[i].ap, other, own, ALU.is_ge))
            yield
            ties.wait(c, d, tri_there)
            f = ties.make(tie_made, lambda e: e.tensor_tensor(over[i].ap, over[i].ap, upper[:, :, :, :], ALU.mult))
            h = ties.make(tie_made, lambda e: e.tensor_tensor(least[i].ap, least[i].ap, lower[:, :, :, :], ALU.mult))
            ties.wait(f, h)
            k = ties.make(tie_made, lambda e: e.tensor_tensor(over[i].ap, over[i].ap, least[i].ap, ALU.add))
            yield
            yield
            dve.wait(k)
            r = dve.make(rank_made, lambda e: e.reduce_sum(rank[i].ap, over[i].ap, X))
            over[i].readers = [r]
            yield
            dve.wait(r)
            ch = dve.make(chosen_made, lambda e: e.tensor_scalar(chosen[i].ap, rank[i].ap, float(TOP_K), None, ALU.is_lt))
            yield
            dve.wait(ch)
            dve.wait(*s1[i].readers)
            s1_there[g] = dve.make(s1_made, lambda e: e.tensor_tensor(s1[i].ap, chosen[i].ap, sig[i].ap, ALU.mult))
            sig[i].readers = [s1_there[g]]
            yield
            dve.wait(s1_there[g])
            dve.wait(*s2[i].readers)
            s2_there[g] = dve.make(s2_made, lambda e: e.tensor_tensor(s2[i].ap, s1[i].ap, s1[i].ap, ALU.mult))
            yield

        hid_there = {}

        def layer1(g, u):
            nonlocal units, hid_count
            t, half = u // HALVES, u % HALVES
            n = GROUPS + g
            hi, lo = nT_hi[n % 2], nT_lo[n % 2]
            at = slice(t * TILE, (t + 1) * TILE)
            up, gt = up_banks[units % 2], gate_banks[units % 2]
            units += 1
            pe.wait(*nT_there[n], *all_weights)
            ready = []
            for m, (bank, made) in enumerate(((up, up_done), (gt, gate_done))):
                c = W13 + (half * 2 + m) * PER_HALF * DIM
                w = slice(c, c + PER_HALF * DIM)
                pe.wait(*bank.readers)
                ready.append(run(pe, passes((hi.ap[:, at], lo.ap[:, at]), (w_hi[:, w], w_lo[:, w]), bank.ap), made))
            if u == TILES * HALVES - 1:
                hi.readers = lo.readers = [ready[1]]
            ac, hd = act[act_turn()], hid[hid_count % len(hid)]
            hid_count += 1
            act_q.wait(ready[0], s1_there[g])
            act_q.wait(*ac.readers)
            for j in range(PER_HALF):
                e_ = half * PER_HALF + j
                silu = act_q.make(act_made, lambda e, j=j, e_=e_: e.activation(
                    ac.ap[:, j, :], up.ap[:, j * DIM:(j + 1) * DIM], ACT.Silu, scale=s1[g % 2].ap[:, t, e_:e_ + 1]))
            up.readers = [silu]
            s1[g % 2].readers = [silu]
            dve.wait(silu, ready[1])
            dve.wait(*hd.readers)
            prod = dve.make(prod_made, lambda e: e.tensor_tensor(
                hd.ap, ac.ap, gt.ap.rearrange("p (j d) -> p j d", j=PER_HALF), ALU.mult))
            ac.readers = gt.readers = [prod]
            drip()
            pool.wait(prod, s2_there[g])
            es = slice(half * PER_HALF, (half + 1) * PER_HALF)
            hid_there[g, u] = pool.make(hid_made, lambda e: e.tensor_tensor(
                hd.ap, hd.ap, s2[g % 2].ap[:, t, es].unsqueeze(2).to_broadcast([P, PER_HALF, DIM]), ALU.mult))
            s2[g % 2].readers = [hid_there[g, u]]
            waiting.append((hd, hid_there[g, u], slice(half * PER_HALF, (half + 1) * PER_HALF), at, g, u))

        waiting, turned_count = [], 0
        hT_there = {}

        def turn_hidden():
            nonlocal turned_count
            hd, there, slots, at, g, unit = waiting.pop(0)
            bank = hT_banks[turned_count % 2]
            turned_count += 1
            pe.wait(there)
            pe.wait(*bank.readers)
            turned = run(pe, [lambda e, j=j: e.transpose(bank.ap[:, j * TILE:(j + 1) * TILE], hd.ap[:, j, :], ident[:, :])
                              for j in range(4)], hT_done)
            hd.readers = [turned]
            hi, lo, src = hT_hi[g % 2], hT_lo[g % 2], bank.ap
            if at is None:
                hi_ap, lo_ap = hi.ap[:, slots, :], lo.ap[:, slots, :]
            else:
                hi_ap, lo_ap, src = hi.ap[:, slots, at], lo.ap[:, slots, at], src.rearrange("p (j c) -> p j c", j=PER_HALF)
            act_q.wait(*attention_over, *hi.readers)
            dve.wait(*attention_over, *lo.readers)
            pair = split(act_q, dve, [turned], src, hi_ap, lo_ap, hT_hi_made, hT_lo_made)
            bank.readers = [pair[1]]
            hT_there[g, unit] = pair
            drip()
            drip()

        yT_there = {}

        def layer2(g, places):
            order = ([SHARED] + list(range(EXPERTS)))[places.start:places.stop]
            if order[0] == SHARED:
                pe.wait(*y_bank.readers)
            hi, lo = hT_hi[g % 2], hT_lo[g % 2]
            for e_ in order:
                last_unit = SHARED if e_ == SHARED else (TILES - 1) * HALVES + e_ // PER_HALF
                pe.wait(*hT_there[g, last_unit])
                c = WSH2 if e_ == SHARED else W2 + e_ * DIM
                w = slice(c, c + DIM)
                steps = passes((w_hi[:, w], w_lo[:, w]), (hi.ap[:, e_, :], lo.ap[:, e_, :]), y_bank.ap,
                               first=(e_ == SHARED), last=(e_ == EXPERTS - 1))
                done = run(pe, steps, y_done)
            if order[-1] != EXPERTS - 1:
                return
            hi.readers = lo.readers = [done]
            act_q.wait(done, tanh_there)
            act_q.wait(*y_sb[0].readers)
            yT_there[g] = act_q.make(y_made, lambda e: e.activation(y_sb[0].ap, y_bank.ap, ACT.Copy, scale=gate_t[:, 1:2]))
            y_bank.readers = [yT_there[g]]

        def finish(g):
            pe.wait(yT_there[g])
            pe.wait(*side_bank.readers)
            turned = run(pe, [lambda e, t=t: e.transpose(side_bank.ap[:, t * DIM:(t + 1) * DIM],
                                                         y_sb[0].ap[:, t * TILE:(t + 1) * TILE], ident[:, :])
                              for t in range(TILES)], yT_done)
            y_sb[0].readers = [turned]
            dve.wait(turned, normed_there[GROUPS + g])
            made = dve.make(result_made, lambda e: e.tensor_tensor(
                row_of(g), row_of(g), side_bank.ap.rearrange("p (t d) -> p t d", t=TILES), ALU.add))
            side_bank.readers = [made]
            sp.wait(made)
            return sp.make(stored, lambda e: e.dma_start(out_tiles[:, TILES * g:TILES * (g + 1), :], row_of(g)), 16)

        def prepare(g, part):
            if g >= GROUPS:
                return
            n = GROUPS + g
            if part == "norm":
                chores.append(norm_stats(n, g, [rows_there[g]]))
                chores.append(norm_apply(n, g))
            elif part == "turn":
                if n in nT_turned:
                    return
                drain_chores()
                norm_turn(n, side_bank)
                norm_split(n, side_bank)
            elif part == "shared 0":
                shared_layer1(g, 0)
            elif part == "shared 1":
                shared_layer1(g, 1)
                chores.append(route(g, pool if g else dve))
                waiting.append((sh_hid[g % 2], sh_hid_there[g], SHARED, None, g, SHARED))

        NORMED = GROUPS + 2
        has = lambda g: 0 <= g < GROUPS
        for s in range(GROUPS + 4):
            if s + 2 < GROUPS:
                load_x(s + 2)
                load_ctx(s + 2)
            if has(s - 3) and s < NORMED:
                chores.append(normalise(s - 3))
                drip()
            stage = norm_stats(s, s % GROUPS, [x_there[s] if has(s) else rows_there[s - GROUPS]]) if s < NORMED else ()
            for _ in stage:
                drip()
            if s != NORMED:
                drain_chores()
            if has(s - 4):
                attend(s - 4)
            drain_chores()
            if 1 <= s <= NORMED:
                turn_bank = nT_bank if s < NORMED else side_bank
                norm_turn(s - 1, turn_bank)
                (norm_copy if has(s - 1) else norm_split)(s - 1, turn_bank)
            if has(s - 2):
                make_scores(s - 2)
                mask_scores(s - 2)
            if has(s):
                split_ctx(s)
            if has(s - 1):
                project_kv(s - 1)
            if has(s - 3):
                turn_probs(s - 3)
            if has(s - 2):
                exponents(s - 2)
            if has(s - 1):
                project_q(s - 1)
            if s == 0:
                wk_split = split(dve, dve, [qkv_there], qkv_raw[:, DIM:2 * DIM], wk_hi[:, :], wk_lo[:, :],
                                 wk_split_hi, wk_split_lo)
                dve.wait(tanh_there, own_there)
                gate_own_there = dve.make(gate_own_made, lambda e: e.tensor_scalar(
                    gate_own[:, :], own_half[:, :], gate_t[:, 0:1], None, ALU.mult))
            if s < NORMED:
                finish_chore(norm_apply(s, s % GROUPS))
            if s == GROUPS + 1:
                finish_chore(normalise(GROUPS - 1))
                for part in ("shared 0", "shared 1"):
                    prepare(0, part)
            if 1 <= s and (s - 1) * W_CHUNK < WCOLS:
                split_weights(s - 1)
                all_weights[:] = [m for pair in w_split.values() for m in pair]

        attention_over += [q_there[GROUPS - 1], scores_ready[GROUPS - 1], exp_there[GROUPS - 1], diag_there[GROUPS - 1],
                           diagT_there[GROUPS - 1], rows_there[GROUPS - 1]] + all_weights

        PREPARE = {1: (1, "turn"), 2: (1, "shared 0"), 3: (1, "shared 1"), 5: (2, "norm")}
        LAYER2 = {1: range(0, 1), 2: range(1, 3), 3: range(3, 4), 4: range(4, 6), 5: range(6, 7), 6: range(7, 9)}
        FINISH = 7
        for g in range(GROUPS):
            for u in range(TILES * HALVES):
                layer1(g, u)
                if g and u in LAYER2:
                    layer2(g - 1, LAYER2[u])
                if g and u == FINISH:
                    finish(g - 1)
                if u in PREPARE:
                    ahead, part = PREPARE[u]
                    prepare(g + ahead, part)
                while len(waiting) > 2:
                    turn_hidden()
            while g + 1 < GROUPS and g + 1 not in s2_there:
                drip()
        while len(waiting) > 1:
            turn_hidden()
        layer2(GROUPS - 1, range(0, 1))
        turn_hidden()
        layer2(GROUPS - 1, range(1, EXPERTS + 1))
        all_stored = finish(GROUPS - 1)
        sp.wait(all_stored)

        block = stack.enter_context(nc.Block())
        block.sync(sp.play)
        block.tensor(pe.play)
        block.vector(dve.play)
        block.scalar(act_q.play)
        block.gpsimd(pool.play)


def kernel(**inputs):
    import concourse.bacc as bacc
    from concourse.bass_utils import run_bass_kernel_spmd

    a = {k: np.asarray(v) for k, v in inputs.items()}
    down = lambda w: w.transpose(2, 0, 1)
    w1, w3 = (down(a[f"L0_ffn_w{i}"]).reshape(DIM, HALVES, PER_HALF * DIM) for i in (1, 3))
    w13 = np.stack([w1, w3], axis=2).reshape(DIM, -1)
    w_moe = np.concatenate([w13, down(a["L0_ffn_w2"]).reshape(DIM, -1), a["L0_ffn_sw1"].T, a["L0_ffn_sw3"].T,
                            a["L0_ffn_gate_w"].T, a["L0_ffn_sw2"].T], axis=1)
    arrays = {
        "x": a["x"].reshape(TOKENS, DIM),
        "ctx_t": a["ctx_1024"].reshape(TOKENS, DIM).T,
        "mask": a["mask_BxSxS2_bk1"].reshape(TOKENS // TILE, TILE, SEQ).transpose(1, 0, 2),
        "w_qkv": np.concatenate([a[f"L0_xattn_W{n}"].T for n in "qkv"], axis=1),
        "b_qk": np.stack([a["L0_xattn_bq"], a["L0_xattn_bk"]], axis=1),
        "bv_row": a["L0_xattn_bv"].reshape(1, DIM),
        "bias_row": a["L0_ffn_expert_bias"].reshape(1, EXPERTS),
        "gates": np.stack([a["g_xattn"], a["g_ffn"]], axis=1),
        "w_moe": w_moe,
    }
    arrays = {k: np.ascontiguousarray(v) for k, v in arrays.items()}
    nc = bacc.Bacc("TRN2", target_bir_lowering=False, num_devices=1)
    aps = [nc.dram_tensor(k, v.shape, mybir.dt.from_np(v.dtype), kind="ExternalInput").ap() for k, v in arrays.items()]
    out = nc.dram_tensor("out", (TOKENS, DIM), F32, kind="ExternalOutput").ap()
    build(nc, *aps, out)
    r = run_bass_kernel_spmd(nc, [arrays], core_ids=[0])
    return r.results[0]["out"].reshape(BATCHES, SEQ, DIM)
```
